# Optimizing a Trainium2 kernel written in Bass

```python
import numpy as np
import jax
import jax.numpy as jnp

def _softmax(x, axis=-1):
    return jax.nn.softmax(x, axis=axis)

def _gelu(x):
    return jax.nn.gelu(x, approximate=True)

def _silu(x):
    return jax.nn.silu(x)

def _sigmoid(x):
    return jax.nn.sigmoid(x)

def _layernorm(x, axis=-1, eps=1e-05):
    m = jnp.mean(x, axis=axis, keepdims=True)
    v = jnp.var(x, axis=axis, keepdims=True)
    return (x - m) / jnp.sqrt(v + eps)

def _scatter_add(tgt, idx, src, axis=0):
    return tgt.at[idx].add(src)

def _segment_sum(src, seg, n):
    return jax.ops.segment_sum(src, seg, n)
kernel_name = 'mk_perceiver_d2_seqx_r4_52f1ef'

def setup_inputs(seed: int=0):
    np.random.seed(seed)
    _w = jnp.asarray

    def _rec_inputs():
        import jax
        import jax.numpy as jnp
        _rk = jax.random.key(seed)
        x = -0.0002928 + 1 * jax.random.normal(jax.random.fold_in(_rk, 1), (8, 64, 256), jnp.float32)
        _lenS = 64 - jax.random.randint(jax.random.fold_in(_rk, 7), (8,), 0, max(1, 64 // 4) + 1, jnp.int32)
        _lenS2 = 1024 - jax.random.randint(jax.random.fold_in(_rk, 8), (8,), 0, max(1, 1024 // 4) + 1, jnp.int32)
        _ctx_1024P = jax.random.normal(jax.random.fold_in(_rk, 11), (8, 16, 256), jnp.float32)
        _ctx_1024c = jax.random.dirichlet(jax.random.fold_in(_rk, 511), 0.3 * jnp.ones((16,), jnp.float32), (8, 1024))
        _ctx_1024t = jnp.einsum('bsk,bkd->bsd', _ctx_1024c, _ctx_1024P)
        _ctx_1024t = _ctx_1024t * jax.lax.rsqrt(jnp.mean(jnp.square(_ctx_1024t)) + 1e-12) * 0.953939
        ctx_1024 = -1.39393e-06 + 0.999914 * (_ctx_1024t + 0.3 * jax.random.normal(jax.random.fold_in(_rk, 611), (8, 1024, 256), jnp.float32))
        _validS = jnp.arange(64)[None, :] < _lenS[:, None]
        _validS2 = jnp.arange(1024)[None, :] < _lenS2[:, None]
        _causal = jnp.tril(jnp.ones((64, 64), dtype=bool))
        mask_BxSxS2_bk0 = jnp.logical_not(jnp.broadcast_to(_validS2[:, None, :], (8, 64, 1024)))
        return (x, ctx_1024, mask_BxSxS2_bk0)
    x, ctx_1024, mask_BxSxS2_bk0 = _rec_inputs()

    def _L0_xattn_setup():
        import jax, jax.numpy as jnp
        import numpy as np
        from math import sqrt
        B, Q, S, D, H = (2, 512, 512, 256, 16)
        ADIM = D // H
        IEPS = 1e-32

        def sparse_norm(scores, nbias):
            t = jax.nn.relu(scores + nbias[0])
            t = t * t
            return t / (t.sum(-1, keepdims=True) + IEPS)
        key = jax.random.key(seed)
        ks = jax.random.split(key, 7)
        sc = 0.02
        return {'iQ': jax.random.normal(ks[0], (B, Q, D), jnp.float32), 'iK': jax.random.normal(ks[1], (B, S, D), jnp.float32), 'mask': jax.random.randint(ks[2], (B, Q, S), 0, 2) > 0, 'Wq': jax.random.normal(ks[3], (D, D), jnp.float32) * sc, 'Wkv': jax.random.normal(ks[4], (2 * D, D), jnp.float32) * sc, 'Wo': jax.random.normal(ks[5], (D, D), jnp.float32) * sc, 'nbias': jnp.zeros((1,), jnp.float32)}
    _L0_xattn_all = _L0_xattn_setup()
    _L0_xattn_in = {k: v for k, v in _L0_xattn_all.items() if k in ('Wq', 'Wkv', 'Wo', 'nbias')}
    del _L0_xattn_all

    def _L0_attn_setup():
        import jax, jax.numpy as jnp
        import numpy as np
        DIM = 256
        STATE = 256
        BATCH, SEQ = (4, 1024)
        key = jax.random.key(seed)
        ks = jax.random.split(key, 12)
        s = 1.0 / np.sqrt(DIM)
        s4 = 1.0 / np.sqrt(DIM // 4)
        ss = 1.0 / np.sqrt(STATE)
        inp = {'x': jax.random.normal(ks[0], (BATCH, SEQ, DIM), dtype=jnp.float32), 'W_B': jax.random.uniform(ks[1], (DIM, STATE), minval=-s, maxval=s), 'b_B': jax.random.uniform(ks[2], (STATE,), minval=-s, maxval=s), 'W_C': jax.random.uniform(ks[3], (DIM, STATE), minval=-s, maxval=s), 'b_C': jax.random.uniform(ks[4], (STATE,), minval=-s, maxval=s), 'W_dt1': jax.random.uniform(ks[5], (DIM, DIM // 4), minval=-s, maxval=s), 'b_dt1': jax.random.uniform(ks[6], (DIM // 4,), minval=-s, maxval=s), 'W_dt2': jax.random.uniform(ks[7], (DIM // 4, STATE), minval=-s4, maxval=s4), 'b_dt2': jnp.full((STATE,), -4.0, dtype=jnp.float32), 'omega_base': jax.random.normal(ks[8], (STATE,)) * 0.1, 'D': jnp.ones((DIM,), dtype=jnp.float32), 'W_out': jax.random.uniform(ks[9], (STATE, DIM), minval=-ss, maxval=ss), 'b_out': jax.random.uniform(ks[10], (DIM,), minval=-ss, maxval=ss)}
        return inp
    _L0_attn_all = _L0_attn_setup()
    _L0_attn_in = {k: v for k, v in _L0_attn_all.items() if k in ('W_B', 'b_B', 'W_C', 'b_C', 'W_dt1', 'b_dt1', 'W_dt2', 'b_dt2', 'omega_base', 'D', 'W_out', 'b_out')}
    del _L0_attn_all

    def _L0_ffn_setup():
        import jax, jax.numpy as jnp
        import numpy as np
        import math
        D = 256
        H = 16
        E = 8
        TOPK = 2
        LAT = D // 2
        KPH = LAT // H
        HD = D // H

        def _forward(hs, q_w, q_b, k_w, k_b, v_w, v_b, o_w, o_b, router_w, router_b, w1, b1, w2, b2):
            B, S, _ = hs.shape
            Q = (hs @ q_w + q_b).reshape(B, S, H, HD).transpose(0, 2, 1, 3)
            K = (hs @ k_w + k_b).reshape(B, S, H, KPH).transpose(0, 2, 1, 3)
            V = (hs @ v_w + v_b).reshape(B, S, H, KPH).transpose(0, 2, 1, 3)
            scores = jnp.einsum('bhsk,bhtk->bhst', Q[..., :KPH], K) / math.sqrt(KPH)
            attn = jax.nn.softmax(scores, axis=-1)
            ao = jnp.einsum('bhst,bhtv->bhsv', attn, V)
            ao = ao.transpose(0, 2, 1, 3).reshape(B, S, H * KPH)
            ao = jnp.concatenate([ao, jnp.zeros((B, S, D - LAT), ao.dtype)], axis=-1)
            mla_out = ao @ o_w + o_b
            probs = jax.nn.softmax(mla_out @ router_w + router_b, axis=-1)
            topw, topi = jax.lax.top_k(probs, TOPK)
            topw = topw / (topw.sum(-1, keepdims=True) + 1e-08)
            combine = jnp.sum(jax.nn.one_hot(topi, E, dtype=probs.dtype) * topw[..., None], axis=-2)
            h1 = jnp.einsum('bsd,edf->ebsf', mla_out, w1) + b1[:, None, None, :]
            h1 = jax.nn.gelu(h1, approximate=False)
            h2 = jnp.einsum('ebsf,efd->ebsd', h1, w2) + b2[:, None, None, :]
            moe_out = jnp.einsum('bse,ebsd->bsd', combine, h2)
            return hs + 0.3 * moe_out
        key = jax.random.key(seed)
        ks = jax.random.split(key, 16)
        s = 0.02
        inp = {'hidden_states': jax.random.normal(ks[0], (2, 512, D), jnp.float32), 'q_w': jax.random.normal(ks[1], (D, D), jnp.float32) * s, 'q_b': jnp.zeros((D,), jnp.float32), 'k_w': jax.random.normal(ks[2], (D, LAT), jnp.float32) * s, 'k_b': jnp.zeros((LAT,), jnp.float32), 'v_w': jax.random.normal(ks[3], (D, LAT), jnp.float32) * s, 'v_b': jnp.zeros((LAT,), jnp.float32), 'o_w': jax.random.normal(ks[4], (D, D), jnp.float32) * s, 'o_b': jnp.zeros((D,), jnp.float32), 'router_w': jax.random.normal(ks[5], (D, E), jnp.float32) * s, 'router_b': jnp.zeros((E,), jnp.float32), 'w1': jax.random.normal(ks[6], (E, D, 2 * D), jnp.float32) * s, 'b1': jnp.zeros((E, 2 * D), jnp.float32), 'w2': jax.random.normal(ks[7], (E, 2 * D, D), jnp.float32) * s, 'b2': jnp.zeros((E, D), jnp.float32)}
        return inp
    _L0_ffn_all = _L0_ffn_setup()
    _L0_ffn_in = {k: v for k, v in _L0_ffn_all.items() if k in ('q_w', 'q_b', 'k_w', 'k_b', 'v_w', 'v_b', 'o_w', 'o_b', 'router_w', 'router_b', 'w1', 'b1', 'w2', 'b2')}
    del _L0_ffn_all

    def _L1_xattn_setup():
        import jax, jax.numpy as jnp
        import numpy as np
        HIDDEN = 256
        HEADS = 16
        HEAD_DIM = 64
        key = jax.random.key(seed)
        ks = jax.random.split(key, 7)
        B, Q, K = (2, 512, 1024)
        s = 1.0 / np.sqrt(HIDDEN)
        return {'query': jax.random.normal(ks[0], (B, Q, HIDDEN), dtype=jnp.float32), 'key': jax.random.normal(ks[1], (B, K, HIDDEN), dtype=jnp.float32), 'value': jax.random.normal(ks[2], (B, K, HIDDEN), dtype=jnp.float32), 'w_q': jax.random.normal(ks[3], (HIDDEN, HEADS * HEAD_DIM), dtype=jnp.float32) * s, 'w_k': jax.random.normal(ks[4], (HIDDEN, HEADS * HEAD_DIM), dtype=jnp.float32) * s, 'w_v': jax.random.normal(ks[5], (HIDDEN, HEADS * HEAD_DIM), dtype=jnp.float32) * s, 'w_o': jax.random.normal(ks[6], (HEADS * HEAD_DIM, HIDDEN), dtype=jnp.float32) * s}
    _L1_xattn_all = _L1_xattn_setup()
    _L1_xattn_in = {k: v for k, v in _L1_xattn_all.items() if k in ('w_q', 'w_k', 'w_v', 'w_o')}
    del _L1_xattn_all

    def _L1_attn_setup():
        import jax, jax.numpy as jnp
        import numpy as np
        HIDDEN, HEADS, HDIM = (256, 8, 64)
        B, S = (4, 2048)
        LN_EPS = 1e-06
        key = jax.random.key(seed)
        ks = jax.random.split(key, 12)
        inner = HEADS * HDIM
        sd = HIDDEN ** (-0.5)
        return {'x': jax.random.normal(ks[0], (B, S, HIDDEN), jnp.float32), 'Wq': jax.random.normal(ks[1], (HIDDEN, inner), jnp.float32) * sd, 'bq': jnp.zeros((inner,), jnp.float32), 'Wk': jax.random.normal(ks[2], (HIDDEN, inner), jnp.float32) * sd, 'bk': jnp.zeros((inner,), jnp.float32), 'Wv': jax.random.normal(ks[3], (HIDDEN, inner), jnp.float32) * sd, 'bv': jnp.zeros((inner,), jnp.float32), 'Wo': jax.random.normal(ks[4], (inner, HIDDEN), jnp.float32) * inner ** (-0.5), 'bo': jnp.zeros((HIDDEN,), jnp.float32), 'alpha': jnp.ones((HEADS, HDIM), jnp.float32), 'aug_param': jax.random.normal(ks[5], (1, HEADS, HDIM), jnp.float32), 'ln_scale': jnp.ones((HIDDEN,), jnp.float32), 'ln_bias': jnp.zeros((HIDDEN,), jnp.float32)}
    _L1_attn_all = _L1_attn_setup()
    _L1_attn_in = {k: v for k, v in _L1_attn_all.items() if k in ('Wq', 'bq', 'Wk', 'bk', 'Wv', 'bv', 'Wo', 'bo', 'alpha', 'aug_param', 'ln_scale', 'ln_bias')}
    del _L1_attn_all

    def _L1_ffn_setup():
        import jax, jax.numpy as jnp
        import numpy as np
        D_MODEL = 256
        D_HIDDEN = 1024
        NUM_EXPERTS = 8
        B, T = (2, 512)
        key = jax.random.key(seed)
        ks = jax.random.split(key, 8)
        s = 0.02
        x = jax.random.normal(ks[0], (B, T, D_MODEL), dtype=jnp.float32)
        Wg = jax.random.normal(ks[1], (D_MODEL, NUM_EXPERTS), dtype=jnp.float32) * s
        bg = jnp.zeros((NUM_EXPERTS,), dtype=jnp.float32)
        W1 = jax.random.normal(ks[2], (NUM_EXPERTS, D_MODEL, D_HIDDEN), dtype=jnp.float32) * s
        b1 = jnp.zeros((NUM_EXPERTS, D_HIDDEN), dtype=jnp.float32)
        W2 = jax.random.normal(ks[3], (NUM_EXPERTS, D_HIDDEN, D_MODEL), dtype=jnp.float32) * s
        b2 = jnp.zeros((NUM_EXPERTS, D_MODEL), dtype=jnp.float32)
        return {'x': x, 'Wg': Wg, 'bg': bg, 'W1': W1, 'b1': b1, 'W2': W2, 'b2': b2}
    _L1_ffn_all = _L1_ffn_setup()
    _L1_ffn_in = {k: v for k, v in _L1_ffn_all.items() if k in ('Wg', 'bg', 'W1', 'b1', 'W2', 'b2')}
    del _L1_ffn_all
    return {'x': x, 'ctx_1024': ctx_1024, 'mask_BxSxS2_bk0': mask_BxSxS2_bk0, 'L0_xattn_Wq': _L0_xattn_in['Wq'], 'L0_xattn_Wkv': _L0_xattn_in['Wkv'], 'L0_xattn_Wo': _L0_xattn_in['Wo'], 'L0_xattn_nbias': _L0_xattn_in['nbias'], 'L0_attn_W_B': _L0_attn_in['W_B'], 'L0_attn_b_B': _L0_attn_in['b_B'], 'L0_attn_W_C': _L0_attn_in['W_C'], 'L0_attn_b_C': _L0_attn_in['b_C'], 'L0_attn_W_dt1': _L0_attn_in['W_dt1'], 'L0_attn_b_dt1': _L0_attn_in['b_dt1'], 'L0_attn_W_dt2': _L0_attn_in['W_dt2'], 'L0_attn_b_dt2': _L0_attn_in['b_dt2'], 'L0_attn_omega_base': _L0_attn_in['omega_base'], 'L0_attn_D': _L0_attn_in['D'], 'L0_attn_W_out': _L0_attn_in['W_out'], 'L0_attn_b_out': _L0_attn_in['b_out'], 'L0_ffn_q_w': _L0_ffn_in['q_w'], 'L0_ffn_q_b': _L0_ffn_in['q_b'], 'L0_ffn_k_w': _L0_ffn_in['k_w'], 'L0_ffn_k_b': _L0_ffn_in['k_b'], 'L0_ffn_v_w': _L0_ffn_in['v_w'], 'L0_ffn_v_b': _L0_ffn_in['v_b'], 'L0_ffn_o_w': _L0_ffn_in['o_w'], 'L0_ffn_o_b': _L0_ffn_in['o_b'], 'L0_ffn_router_w': _L0_ffn_in['router_w'], 'L0_ffn_router_b': _L0_ffn_in['router_b'], 'L0_ffn_w1': _L0_ffn_in['w1'], 'L0_ffn_b1': _L0_ffn_in['b1'], 'L0_ffn_w2': _L0_ffn_in['w2'], 'L0_ffn_b2': _L0_ffn_in['b2'], 'L1_xattn_w_q': _L1_xattn_in['w_q'], 'L1_xattn_w_k': _L1_xattn_in['w_k'], 'L1_xattn_w_v': _L1_xattn_in['w_v'], 'L1_xattn_w_o': _L1_xattn_in['w_o'], 'L1_attn_Wq': _L1_attn_in['Wq'], 'L1_attn_bq': _L1_attn_in['bq'], 'L1_attn_Wk': _L1_attn_in['Wk'], 'L1_attn_bk': _L1_attn_in['bk'], 'L1_attn_Wv': _L1_attn_in['Wv'], 'L1_attn_bv': _L1_attn_in['bv'], 'L1_attn_Wo': _L1_attn_in['Wo'], 'L1_attn_bo': _L1_attn_in['bo'], 'L1_attn_alpha': _L1_attn_in['alpha'], 'L1_attn_aug_param': _L1_attn_in['aug_param'], 'L1_attn_ln_scale': _L1_attn_in['ln_scale'], 'L1_attn_ln_bias': _L1_attn_in['ln_bias'], 'L1_ffn_Wg': _L1_ffn_in['Wg'], 'L1_ffn_bg': _L1_ffn_in['bg'], 'L1_ffn_W1': _L1_ffn_in['W1'], 'L1_ffn_b1': _L1_ffn_in['b1'], 'L1_ffn_W2': _L1_ffn_in['W2'], 'L1_ffn_b2': _L1_ffn_in['b2']}

def reference(x, ctx_1024, mask_BxSxS2_bk0, L0_xattn_Wq, L0_xattn_Wkv, L0_xattn_Wo, L0_xattn_nbias, L0_attn_W_B, L0_attn_b_B, L0_attn_W_C, L0_attn_b_C, L0_attn_W_dt1, L0_attn_b_dt1, L0_attn_W_dt2, L0_attn_b_dt2, L0_attn_omega_base, L0_attn_D, L0_attn_W_out, L0_attn_b_out, L0_ffn_q_w, L0_ffn_q_b, L0_ffn_k_w, L0_ffn_k_b, L0_ffn_v_w, L0_ffn_v_b, L0_ffn_o_w, L0_ffn_o_b, L0_ffn_router_w, L0_ffn_router_b, L0_ffn_w1, L0_ffn_b1, L0_ffn_w2, L0_ffn_b2, L1_xattn_w_q, L1_xattn_w_k, L1_xattn_w_v, L1_xattn_w_o, L1_attn_Wq, L1_attn_bq, L1_attn_Wk, L1_attn_bk, L1_attn_Wv, L1_attn_bv, L1_attn_Wo, L1_attn_bo, L1_attn_alpha, L1_attn_aug_param, L1_attn_ln_scale, L1_attn_ln_bias, L1_ffn_Wg, L1_ffn_bg, L1_ffn_W1, L1_ffn_b1, L1_ffn_W2, L1_ffn_b2):
    import jax
    import jax.numpy as jnp

    def _L0_xattn_ref(iQ, iK, mask, Wq, Wkv, Wo, nbias):
        import jax, jax.numpy as jnp
        import numpy as np
        from math import sqrt
        B, Q, S, D, H = (2, 512, 512, 256, 16)
        ADIM = D // H
        IEPS = 1e-32

        def sparse_norm(scores, nbias):
            t = jax.nn.relu(scores + nbias[0])
            t = t * t
            return t / (t.sum(-1, keepdims=True) + IEPS)
        b, q, _ = iQ.shape
        s = iK.shape[1]
        rq = (iQ @ Wq.T).reshape(b, q, H, ADIM)
        kv = (iK @ Wkv.T).reshape(b, s, 2, H, ADIM)
        rk, rv = (kv[:, :, 0], kv[:, :, 1])
        scores = jnp.einsum('bqhd,bshd->bhqs', rq, rk) / sqrt(ADIM)
        scores = jnp.where(mask[:, None, :, :], jnp.float32(-1e+32), scores)
        attn = sparse_norm(scores, nbias)
        o = jnp.einsum('bhqs,bshd->bqhd', attn, rv).reshape(b, q, H * ADIM)
        return o @ Wo.T

    def _L0_attn_ref(x, W_B, b_B, W_C, b_C, W_dt1, b_dt1, W_dt2, b_dt2, omega_base, D, W_out, b_out):
        import jax, jax.numpy as jnp
        import numpy as np
        DIM = 256
        STATE = 256
        BATCH, SEQ = (4, 1024)
        Bm = x @ W_B + b_B
        Cm = x @ W_C + b_C
        dt = jax.nn.softplus((x @ W_dt1 + b_dt1) @ W_dt2 + b_dt2)
        omega = omega_base * dt
        phi = jnp.cumsum(omega, axis=1)
        content = Bm * x[..., :STATE]
        cphi, sphi = (jnp.cos(phi), jnp.sin(phi))
        memory_real = jnp.cumsum(content * cphi, axis=1)
        memory_imag = jnp.cumsum(content * sphi, axis=1)
        retrieved = Cm * (memory_real * cphi + memory_imag * sphi)
        y = retrieved @ W_out + b_out + D * x
        return y

    def _L0_ffn_ref(hidden_states, q_w, q_b, k_w, k_b, v_w, v_b, o_w, o_b, router_w, router_b, w1, b1, w2, b2):
        import jax, jax.numpy as jnp
        import numpy as np
        import math
        D = 256
        H = 16
        E = 8
        TOPK = 2
        LAT = D // 2
        KPH = LAT // H
        HD = D // H

        def _forward(hs, q_w, q_b, k_w, k_b, v_w, v_b, o_w, o_b, router_w, router_b, w1, b1, w2, b2):
            B, S, _ = hs.shape
            Q = (hs @ q_w + q_b).reshape(B, S, H, HD).transpose(0, 2, 1, 3)
            K = (hs @ k_w + k_b).reshape(B, S, H, KPH).transpose(0, 2, 1, 3)
            V = (hs @ v_w + v_b).reshape(B, S, H, KPH).transpose(0, 2, 1, 3)
            scores = jnp.einsum('bhsk,bhtk->bhst', Q[..., :KPH], K) / math.sqrt(KPH)
            attn = jax.nn.softmax(scores, axis=-1)
            ao = jnp.einsum('bhst,bhtv->bhsv', attn, V)
            ao = ao.transpose(0, 2, 1, 3).reshape(B, S, H * KPH)
            ao = jnp.concatenate([ao, jnp.zeros((B, S, D - LAT), ao.dtype)], axis=-1)
            mla_out = ao @ o_w + o_b
            probs = jax.nn.softmax(mla_out @ router_w + router_b, axis=-1)
            topw, topi = jax.lax.top_k(probs, TOPK)
            topw = topw / (topw.sum(-1, keepdims=True) + 1e-08)
            combine = jnp.sum(jax.nn.one_hot(topi, E, dtype=probs.dtype) * topw[..., None], axis=-2)
            h1 = jnp.einsum('bsd,edf->ebsf', mla_out, w1) + b1[:, None, None, :]
            h1 = jax.nn.gelu(h1, approximate=False)
            h2 = jnp.einsum('ebsf,efd->ebsd', h1, w2) + b2[:, None, None, :]
            moe_out = jnp.einsum('bse,ebsd->bsd', combine, h2)
            return hs + 0.3 * moe_out
        return _forward(hidden_states, q_w, q_b, k_w, k_b, v_w, v_b, o_w, o_b, router_w, router_b, w1, b1, w2, b2)

    def _L1_xattn_ref(query, key, value, w_q, w_k, w_v, w_o):
        import jax, jax.numpy as jnp
        import numpy as np
        HIDDEN = 256
        HEADS = 16
        HEAD_DIM = 64
        B, Q, _ = query.shape
        Kl = key.shape[1]
        scale = HEAD_DIM ** (-0.5)
        q = (query @ w_q).reshape(B, Q, HEADS, HEAD_DIM).transpose(0, 2, 1, 3)
        k = (key @ w_k).reshape(B, Kl, HEADS, HEAD_DIM).transpose(0, 2, 1, 3)
        v = (value @ w_v).reshape(B, Kl, HEADS, HEAD_DIM).transpose(0, 2, 1, 3)
        scores = jnp.einsum('bhqd,bhkd->bhqk', q, k) * scale
        attn = jax.nn.softmax(scores, axis=-1)
        out = jnp.einsum('bhqk,bhkd->bhqd', attn, v)
        out = out.transpose(0, 2, 1, 3).reshape(B, Q, HEADS * HEAD_DIM)
        return out @ w_o

    def _L1_attn_ref(x, Wq, bq, Wk, bk, Wv, bv, Wo, bo, alpha, aug_param, ln_scale, ln_bias):
        import jax, jax.numpy as jnp
        import numpy as np
        HIDDEN, HEADS, HDIM = (256, 8, 64)
        B, S = (4, 2048)
        LN_EPS = 1e-06
        b, s, _ = x.shape
        h, d = alpha.shape
        scale = d ** (-0.5)
        q = (x @ Wq + bq).reshape(b, s, h, d)
        k = (x @ Wk + bk).reshape(b, s, h, d)
        v = (x @ Wv + bv).reshape(b, s, h, d)
        decay = jax.nn.sigmoid(alpha)

        def step(state, qkv):
            q_t, k_t, v_t = qkv
            attn = jax.nn.softmax(jnp.einsum('bhd,bhd->bh', q_t, k_t) * scale, axis=-1)
            new_state = decay * state + (1.0 - decay) * attn[..., None] * v_t
            return (new_state, new_state)
        qs = jnp.moveaxis(q, 1, 0)
        ks_ = jnp.moveaxis(k, 1, 0)
        vs = jnp.moveaxis(v, 1, 0)
        init = jnp.zeros((b, h, d), x.dtype)
        _, states = jax.lax.scan(step, init, (qs, ks_, vs))
        states = jnp.moveaxis(states, 0, 1)
        aug = jax.nn.sigmoid(q * aug_param)
        out = (q * states + aug).reshape(b, s, h * d)
        out = out @ Wo + bo
        mean = jnp.mean(out, axis=-1, keepdims=True)
        var = jnp.var(out, axis=-1, keepdims=True)
        return (out - mean) * jax.lax.rsqrt(var + LN_EPS) * ln_scale + ln_bias

    def _L1_ffn_ref(x, Wg, bg, W1, b1, W2, b2):
        import jax, jax.numpy as jnp
        import numpy as np
        D_MODEL = 256
        D_HIDDEN = 1024
        NUM_EXPERTS = 8
        B, T = (2, 512)
        gate_logits = jnp.einsum('btd,de->bte', x, Wg) + bg
        gate_scores = jax.nn.softmax(gate_logits, axis=-1)
        top1_idx = jnp.argmax(gate_scores, axis=-1)
        top1_mask = jax.nn.one_hot(top1_idx, NUM_EXPERTS, dtype=x.dtype)
        top1_weight = jnp.sum(gate_scores * top1_mask, axis=-1, keepdims=True)
        h = jax.nn.silu(jnp.einsum('btd,edh->bteh', x, W1) + b1)
        o = jnp.einsum('bteh,ehd->bted', h, W2) + b2
        y = jnp.sum(o * top1_mask[..., None], axis=2) * top1_weight
        return y
    x = x + _L0_xattn_ref(_layernorm(x, axis=-1), ctx_1024, mask_BxSxS2_bk0, L0_xattn_Wq, L0_xattn_Wkv, L0_xattn_Wo, L0_xattn_nbias)
    x = x + _L0_attn_ref(_layernorm(x, axis=-1), L0_attn_W_B, L0_attn_b_B, L0_attn_W_C, L0_attn_b_C, L0_attn_W_dt1, L0_attn_b_dt1, L0_attn_W_dt2, L0_attn_b_dt2, L0_attn_omega_base, L0_attn_D, L0_attn_W_out, L0_attn_b_out)
    x = x + _L0_ffn_ref(_layernorm(x, axis=-1), L0_ffn_q_w, L0_ffn_q_b, L0_ffn_k_w, L0_ffn_k_b, L0_ffn_v_w, L0_ffn_v_b, L0_ffn_o_w, L0_ffn_o_b, L0_ffn_router_w, L0_ffn_router_b, L0_ffn_w1, L0_ffn_b1, L0_ffn_w2, L0_ffn_b2)
    x = x + _L1_xattn_ref(_layernorm(x, axis=-1), ctx_1024, ctx_1024, L1_xattn_w_q, L1_xattn_w_k, L1_xattn_w_v, L1_xattn_w_o)
    x = x + _L1_attn_ref(_layernorm(x, axis=-1), L1_attn_Wq, L1_attn_bq, L1_attn_Wk, L1_attn_bk, L1_attn_Wv, L1_attn_bv, L1_attn_Wo, L1_attn_bo, L1_attn_alpha, L1_attn_aug_param, L1_attn_ln_scale, L1_attn_ln_bias)
    x = x + _L1_ffn_ref(_layernorm(x, axis=-1), L1_ffn_Wg, L1_ffn_bg, L1_ffn_W1, L1_ffn_b1, L1_ffn_W2, L1_ffn_b2)
    return x

_drawn_inputs = setup_inputs


def setup_inputs(seed=0):
    import zlib

    import numpy as np

    out = dict(_drawn_inputs(seed))
    spreads = {'L0_attn_b_dt2': (-4.0, 0.6),
     'L0_attn_D': (1.0, 0.2),
     'L0_ffn_q_b': (0.0, 0.8),
     'L0_ffn_k_b': (0.0, 0.8),
     'L0_ffn_v_b': (0.0, 0.8),
     'L0_ffn_o_b': (0.0, 0.8),
     'L0_ffn_router_b': (0.0, 0.8),
     'L0_ffn_b1': (0.0, 0.8),
     'L0_ffn_b2': (0.0, 0.8),
     'L1_attn_bq': (0.0, 0.706),
     'L1_attn_bk': (0.0, 0.8),
     'L1_attn_bv': (0.0, 0.8),
     'L1_attn_bo': (0.0, 0.1),
     'L1_attn_alpha': (1.0, 0.6),
     'L1_attn_ln_scale': (1.0, 0.2),
     'L1_attn_ln_bias': (0.0, 0.293),
     'L1_ffn_bg': (0.0, 0.8),
     'L1_ffn_b1': (0.0, 0.8),
     'L1_ffn_b2': (0.0, 0.8)}
    factors = {'L0_attn_W_dt1': 8.0,
     'L0_attn_b_dt1': 8.0,
     'L0_attn_W_dt2': 8.0,
     'L0_attn_omega_base': 8.0,
     'L0_attn_b_out': 3.801,
     'L0_ffn_q_w': 8.0,
     'L0_ffn_k_w': 8.0,
     'L0_ffn_v_w': 8.0,
     'L0_ffn_o_w': 8.0,
     'L0_ffn_router_w': 8.0,
     'L0_ffn_w1': 8.0,
     'L0_ffn_w2': 8.0,
     'L1_ffn_Wg': 7.637,
     'L1_ffn_W1': 8.0,
     'L1_ffn_W2': 8.0}
    for name, (base, spread) in spreads.items():
        noise = np.random.default_rng([zlib.crc32(name.encode()), seed]).standard_normal(out[name].shape)
        drawn = base * np.exp(spread * noise) if base else spread * noise
        out[name] = jnp.asarray(drawn.astype(out[name].dtype))
    for name, factor in factors.items():
        out[name] = (out[name] * factor).astype(out[name].dtype)
    return out
```

```python
import concourse.bass as bass
from concourse import mybir
from contextlib import ExitStack

F32 = mybir.dt.float32
F32R = mybir.dt.float32r
BF16 = mybir.dt.bfloat16
U8 = mybir.dt.uint8
ALU = mybir.AluOpType
ACT = mybir.ActivationFunctionType
AX = mybir.AxisListType.X

P = 128
B, T, D = 8, 64, 256
NT = B * T
TT = NT // P
DC = D // P
S = 1024
KT = S // P
E = 8
LN_EPS = 1e-5
MAGIC = 12582912.0


def bc(ap, axis, n):
    v = ap.unsqueeze(axis)
    shape = list(v.shape)
    shape[axis] = n
    return v.broadcast_to(shape)


def wait_if_positive(engine, sem, value):
    if not isinstance(value, int) or value > 0:
        engine.wait_ge(sem, value)


def each(engine, count, body):
    body(0)
    with engine.Fori(1, count - 1) as i:
        body(i)
    body(count - 1)


def stepper(engine, sem):
    count = [0]

    def step(ins):
        count[0] += 1
        ins.then_inc(sem, 1)
        engine.wait_ge(sem, count[0])

    return step


class Core:

    def __init__(self, nc, ctx):
        self.nc, self.ctx, self.sems = nc, ctx, []
        self.x = self.sb("resid", [P, TT, D])
        self.xn = self.sb("xn", [P, TT, D])
        self.xnT = self.sb("xnT", [P, DC, NT])
        self.ident = self.sb("ident", [P, P])
        self.stats = self.sb("stats", [P, TT, 6])
        self.meanvar = self.sb("meanvar", [P, TT, 2])
        self.vareps = self.sb("vareps", [P, TT])
        self.std = self.sb("std", [P, TT])
        self.rstd = self.sb("rstd", [P, TT])
        self.newton = self.sb("newton", [P, TT])
        self.ps = [ctx.enter_context(nc.psum_tensor(f"ps{i}", [P, 1024], F32)) for i in range(4)]

    def sb(self, name, shape, dt=F32, ctx=None):
        return (ctx or self.ctx).enter_context(self.nc.sbuf_tensor(name, shape, dt))

    def sem(self, name):
        s = self.nc.alloc_semaphore(name=name)
        self.sems.append(s)
        return s

    def clear_sems(self):
        with self.nc.Block() as block:
            @block.gpsimd
            def _(pool):
                self.nc.clear_and_free_semaphores(self.sems)
        self.sems = []

    def bank(self, i):
        return self.ps[i // 2][:, 512 * (i % 2):512 * (i % 2) + 512]


class Norm:

    def __init__(self, core, tag):
        self.c = core
        self.var = core.sem(tag + "_ln_var")
        self.std = core.sem(tag + "_ln_std")
        self.xn = core.sem(tag + "_xn_ready")
        self.xnT_psum = core.sem(tag + "_xnT_psum")
        self.xnT = core.sem(tag + "_xnT_ready")

    def vector_stats(self, step, src):
        c, nc = self.c, self.c.nc
        for j in range(TT):
            last = nc.vector.bn_stats(c.stats[:, j, :], src[:, j, :])
            step(last)
        for j in range(TT):
            step(nc.vector.bn_aggr(c.meanvar[:, j, :], c.stats[:, j, :]))

    def vector_norm(self, eng, step, src, dst, eps, ready):
        c, nc = self.c, self.c.nc
        self.vector_stats(step, src)
        nc.vector.tensor_scalar(c.vareps[:], c.meanvar[:, :, 1], eps, None, ALU.add).then_inc(self.var, 1)
        eng.wait_ge(self.std, 1)
        step(nc.vector.reciprocal(c.rstd[:], c.std[:]))
        step(nc.vector.tensor_tensor(c.newton[:], c.rstd[:], c.rstd[:], ALU.mult))
        step(nc.vector.tensor_tensor(c.newton[:], c.newton[:], c.vareps[:], ALU.mult))
        step(nc.vector.tensor_scalar(c.newton[:], c.newton[:], -0.5, 1.5, ALU.mult, ALU.add))
        step(nc.vector.tensor_tensor(c.rstd[:], c.rstd[:], c.newton[:], ALU.mult))
        for j in range(TT):
            nc.vector.tensor_scalar(dst[:, j, :], src[:, j, :], c.meanvar[:, j, 0:1], c.rstd[:, j:j + 1],
                                    ALU.subtract, ALU.mult).then_inc(ready, 1)

    def vector(self, eng, step):
        c, nc = self.c, self.c.nc
        self.vector_norm(eng, step, c.x, c.xn, LN_EPS, self.xn)
        eng.wait_ge(self.xnT_psum, TT)
        nc.vector.tensor_copy(c.xnT[:, 1, :], c.bank(1)).then_inc(self.xnT, 1)

    def scalar_std(self, eng):
        c, nc = self.c, self.c.nc
        eng.wait_ge(self.var, 1)
        nc.scalar.activation(c.std[:], c.vareps[:], ACT.Sqrt).then_inc(self.std, 1)

    def scalar(self, eng):
        c, nc = self.c, self.c.nc
        self.scalar_std(eng)
        eng.wait_ge(self.xnT_psum, TT)
        nc.scalar.copy(c.xnT[:, 0, :], c.bank(0)).then_inc(self.xnT, 1)

    def tensor(self, eng):
        c, nc = self.c, self.c.nc
        for j in range(TT):
            eng.wait_ge(self.xn, j + 1)
            for k in range(DC):
                last = nc.tensor.transpose(c.bank(k)[:, j * P:(j + 1) * P], c.xn[:, j, k * P:(k + 1) * P],
                                           c.ident[:])
            last.then_inc(self.xnT_psum, 1)
        eng.wait_ge(self.xnT, DC)


def product3(nc, out, a, b, start, stop, skip=False):
    for n, (i, j) in enumerate(((0, 0), (0, 1), (1, 0))):
        last = nc.tensor.matmul(out, a[i], b[j], start=start and n == 0, stop=stop and n == 2,
                                skip_group_check=skip)
    return last


def xattn0(core, x_d, ctxT_d, maskT_d, wqT_d, wkvT_d, woT_d, nbias_d):
    nc = core.nc
    H, HD = 16, 16
    HO = P // HD
    HP = H // 2
    BIG = -4e32
    UN = KT * DC
    with ExitStack() as ctx:
        sb = lambda name, shape, dt=F32: core.sb("a_" + name, shape, dt, ctx)
        sem = lambda name: core.sem("a_" + name)
        wq = sb("wq", [P, DC, D])
        wkv = sb("wkv", [P, DC, 2 * D])
        wkv_hi, wkv_lo = sb("wkv_hi", [P, DC, 2 * D], F32R), sb("wkv_lo", [P, DC, 2 * D], F32R)
        wo = sb("wo", [P, 2, D])
        nb = sb("nb", [P, 1])
        ctxT = sb("ctxT", [P, DC, S])
        ctxT_hi, ctxT_lo = sb("ctxT_hi", [P, DC, S], F32R), sb("ctxT_lo", [P, DC, S], F32R)
        kT_hi, kT_lo = sb("kT_hi", [P, DC, S], F32R), sb("kT_lo", [P, DC, S], F32R)
        VW = 2 * HD + 1
        v1 = sb("v1", [P, KT, HP, VW])
        qT_hi, qT_lo = sb("qT_hi", [P, DC, NT]), sb("qT_lo", [P, DC, NT])
        qd_hi, qd_lo = sb("qd_hi", [P, DC, HO, T], F32R), sb("qd_lo", [P, DC, HO, T], F32R)
        headmask = sb("headmask", [P, HO])
        mask_u8 = sb("mask_u8", [P, KT, T], U8)
        mask_bf = sb("mask_bf", [P, KT, T], BF16)
        negbig = sb("negbig", [P, P], BF16)
        NU, NP = 3, 4
        u = sb("u", [P, NU, HO * T])
        pr = sb("pr", [P, NP, HO * T])
        rden = sb("rden", [P, HP])
        o = sb("o", [P, B, HP, HD])
        oT = sb("oT", [P, 2, B, T])

        x_in, wkv_in, w_in, const = sem("x_in"), sem("wkv_in"), sem("w_in"), sem("const")
        pool_step, dve_step = sem("pool_step"), sem("dve_step")
        ctx_in, mask_in = sem("ctx_in"), sem("mask_in")
        ctx_hi, ctx_lo = sem("ctx_hi"), sem("ctx_lo")
        w_hi, w_lo = sem("w_hi"), sem("w_lo")
        mask_ready = sem("mask_ready")
        q_psum, q_hi, q_lo = sem("q_psum"), sem("q_hi"), sem("q_lo")
        qd_ready = sem("qd_ready")
        kv_psum, k_hi, k_lo, v_done = sem("kv_psum"), sem("k_hi"), sem("k_lo"), sem("v_done")
        s_psum, u_ready, p_ready, pv = sem("s_psum"), sem("u_ready"), sem("p_ready"), sem("pv")
        r_ready, o_ready = sem("r_ready"), sem("o_ready")
        oT_psum, oT_ready, y_psum, x_out = sem("oT_psum"), sem("oT_ready"), sem("y_psum"), sem("x_out")
        norm = Norm(core, "a")
        ident, x = core.ident, core.x

        block = ctx.enter_context(nc.Block())

        @block.sync
        def _(sp):
            sp.dma_start(x[:], x_d.rearrange("(j p) d -> p j d", p=P)).then_inc(x_in, 16)
            sp.dma_start(wkv[:], wkvT_d.rearrange("(c p) o -> p c o", p=P)).then_inc(wkv_in, 16)

            def load(b):
                sp.dma_start(ctxT[:], ctxT_d[b, :, :].rearrange("(c p) k -> p c k", p=P) if isinstance(b, int)
                             else ctxT_d[bass.ds(b, 1), :, :].rearrange("o (c p) k -> (o p) c k", p=P)
                             ).then_inc(ctx_in, 16)
                sp.dma_start(mask_u8[:], maskT_d[b, :, :].rearrange("p (k t) -> p k t", t=T) if isinstance(b, int)
                             else maskT_d[bass.ds(b, 1), :, :].rearrange("o p (k t) -> (o p) k t", t=T)
                             ).then_inc(mask_in, 16)

            load(0)
            sp.dma_start(wq[:], wqT_d.rearrange("(c p) o -> p c o", p=P)).then_inc(w_in, 16)
            sp.dma_start(wo[:], woT_d.rearrange("(c p) o -> p c o", p=P)).then_inc(w_in, 16)
            sp.dma_start(nb[:], nbias_d.partition_broadcast(P)).then_inc(w_in, 16)
            with sp.Fori(1, B) as b:
                sp.wait_ge(ctx_hi, b)
                sp.wait_ge(ctx_lo, b)
                sp.wait_ge(mask_ready, b)
                load(b)

        @block.gpsimd
        def _(pool):
            step = stepper(pool, pool_step)
            step(nc.gpsimd.memset(ident[:], 0.0))
            nc.gpsimd.affine_select(out=ident[:], in_=ident[:], compare_op=ALU.not_equal, fill=1.0, base=0,
                                    pattern=[[-1, P]], channel_multiplier=1).then_inc(const, 1)
            step(nc.gpsimd.memset(negbig[:], 0.0))
            nc.gpsimd.affine_select(out=negbig[:], in_=negbig[:], compare_op=ALU.not_equal, fill=BIG, base=0,
                                    pattern=[[-1, P]], channel_multiplier=1).then_inc(const, 1)
            step(nc.gpsimd.memset(headmask[:], 1.0))
            step(nc.gpsimd.affine_select(out=headmask[:], in_=headmask[:], compare_op=ALU.is_ge, fill=0.0,
                                         base=0, pattern=[[-HD, HO]], channel_multiplier=1))
            nc.gpsimd.affine_select(out=headmask[:], in_=headmask[:], compare_op=ALU.is_ge, fill=0.0,
                                    base=HD - 1, pattern=[[HD, HO]], channel_multiplier=-1).then_inc(const, 1)
            nc.gpsimd.memset(v1[:], 1.0).then_inc(const, 1)
            pool.wait_ge(w_hi, 1)
            nc.gpsimd.tensor_tensor(wkv_lo[:], wkv[:], wkv_hi[:].bitcast(F32), ALU.subtract).then_inc(w_lo, 1)

            def split(b):
                pool.wait_ge(ctx_hi, b + 1)
                nc.gpsimd.tensor_tensor(ctxT_lo[:], ctxT[:], ctxT_hi[:].bitcast(F32),
                                        ALU.subtract).then_inc(ctx_lo, 1)

            split(0)
            with pool.Fori(1, B) as b:
                split(b)

        @block.scalar
        def _(act):
            act.wait_ge(wkv_in, 16)
            nc.scalar.copy(wkv_hi[:], wkv[:]).then_inc(w_hi, 1)

            def split(b):
                act.wait_ge(ctx_in, 16 * b + 16)
                wait_if_positive(act, kv_psum, 8 * b)
                nc.scalar.copy(ctxT_hi[:], ctxT[:]).then_inc(ctx_hi, 1)

            split(0)
            norm.scalar(act)
            for c in range(DC):
                act.wait_ge(q_psum, c + 1)
                nc.scalar.copy(qT_hi[:, c, :].bitcast(F32R), core.bank(2 + c)).then_inc(q_hi, 1)
            act.wait_ge(w_in, 48)

            def batch(b):
                wait_if_positive(act, s_psum, UN * b)
                for n in range(4):
                    act.wait_ge(kv_psum, 8 * b + n + 1)
                    c, h = n // 2, n % 2
                    nc.scalar.copy(kT_hi[:, c, 512 * h:512 * h + 512], core.bank(4 + n % 2)).then_inc(k_hi, 1)
                wait_if_positive(act, pv, UN * b)
                for n in range(4):
                    act.wait_ge(kv_psum, 8 * b + n + 5)
                    nc.scalar.copy(v1[:, 2 * n:2 * n + 2, :, 0:2 * HD],
                                   core.bank(4 + n % 2).rearrange("p (k h d) -> p k h d", k=2, h=HP)
                                   ).then_inc(v_done, 1)
                if not isinstance(b, int) or b < B - 1:
                    split(b + 1)
                for n in range(UN):
                    act.wait_ge(s_psum, UN * b + n + 1)
                    if n >= NU:
                        act.wait_ge(p_ready, UN * b + n - NU + 1)
                    else:
                        wait_if_positive(act, p_ready, UN * b)
                    nc.scalar.activation(u[:, n % NU, :], core.bank(n % 4), ACT.Relu, bias=nb[:],
                                         scale=HD ** -0.5).then_inc(u_ready, 1)

            each(act, B, batch)
            act.wait_ge(oT_psum, 1)
            oTp = core.ps[0][:].rearrange("p (b h q) -> p h b q", b=B, h=2)
            for h in range(2):
                last = nc.scalar.copy(oT[:, h, :, :], oTp[:, h, :, :])
            last.then_inc(oT_ready, 1)

        @block.vector
        def _(dve):
            step = stepper(dve, dve_step)
            dve.wait_ge(x_in, 16)
            norm.vector(dve, step)
            for c in range(DC):
                dve.wait_ge(q_hi, c + 1)
                nc.vector.tensor_tensor(qT_lo[:, c, :], core.bank(2 + c), qT_hi[:, c, :],
                                        ALU.subtract).then_inc(q_lo, 1)
            dve.wait_ge(q_lo, DC)
            dve.wait_ge(const, 4)
            NUQ = 4

            def batch(b):
                wait_if_positive(dve, s_psum, UN * b)
                dve.wait_ge(mask_in, 16 * b + 16)
                nc.vector.tensor_copy(mask_bf[:], mask_u8[:]).then_inc(mask_ready, 1)
                for c in range(DC):
                    for dst, src in ((qd_hi, qT_hi), (qd_lo, qT_lo)):
                        nc.vector.tensor_tensor(dst[:, c, :, :], bc(src[:, c, bass.ds(b * T, T)], 1, HO),
                                                bc(headmask[:], 2, T), ALU.mult).then_inc(qd_ready, 1)
                for n in range(4):
                    dve.wait_ge(k_hi, 4 * b + n + 1)
                    c, h = n // 2, n % 2
                    nc.vector.tensor_tensor(kT_lo[:, c, 512 * h:512 * h + 512], core.bank(4 + n % 2),
                                            kT_hi[:, c, 512 * h:512 * h + 512].bitcast(F32),
                                            ALU.subtract).then_inc(k_lo, 1)
                for n in range(UN):
                    dve.wait_ge(u_ready, UN * b + n + 1)
                    if n >= NP:
                        dve.wait_ge(pv, UN * b + n - NP + 1)
                    else:
                        wait_if_positive(dve, pv, UN * b)
                    nc.vector.tensor_tensor(pr[:, n % NP, :], u[:, n % NU, :], u[:, n % NU, :],
                                            ALU.mult).then_inc(p_ready, 1)
                dve.wait_ge(pv, UN * b + UN)
                op = core.bank(6)[:, 0:HP * VW].rearrange("p (h w) -> p h w", w=VW)
                nc.vector.tensor_scalar(rden[:], op[:, :, 2 * HD], 1e-32, None, ALU.add).then_inc(r_ready, 1)
                dve.wait_ge(r_ready, 2 * b + 1)
                nc.vector.reciprocal(rden[:], rden[:]).then_inc(r_ready, 1)
                dve.wait_ge(r_ready, 2 * b + 2)
                for h in range(2):
                    half = slice(T * h, T * h + T)
                    nc.vector.tensor_tensor(o[half, bass.ds(b, 1), :, :].rearrange("p o h d -> p (o h) d"),
                                            op[half, :, HD * h:HD * h + HD],
                                            bc(rden[half, :], 2, HD), ALU.mult).then_inc(o_ready, 1)

            each(dve, B, batch)
            for j in range(2):
                dve.wait_ge(y_psum, j + 1)
                nc.vector.tensor_tensor(x[:, 2 * j:2 * j + 2, :], x[:, 2 * j:2 * j + 2, :],
                                        core.bank(2 + j).rearrange("p (j d) -> p j d", d=D),
                                        ALU.add).then_inc(x_out, 1)

        @block.tensor
        def _(pe):
            pe.wait_ge(const, 2)
            norm.tensor(pe)
            pe.wait_ge(w_in, 48)
            for c in range(DC):
                for k in range(DC):
                    last = nc.tensor.matmul(core.bank(2 + c), wq[:, k, c * P:(c + 1) * P], core.xnT[:, k, :],
                                            start=k == 0, stop=k == DC - 1)
                last.then_inc(q_psum, 1)
            pe.wait_ge(w_lo, 1)

            w2 = (wkv_hi, wkv_lo)
            c2 = (ctxT_hi, ctxT_lo)

            def scores(b, n):
                k, c = n // DC, n % DC
                if n >= 4:
                    pe.wait_ge(u_ready, UN * b + n - 3)
                out = core.bank(n % 4)
                product3(nc, out, [t[:, c, k * P:(k + 1) * P] for t in (kT_hi, kT_lo)],
                         [t[:, c, :, :].rearrange("p h t -> p (h t)") for t in (qd_hi, qd_lo)], True, False)
                nc.tensor.matmul(out, negbig[:], bc(mask_bf[:, k, :], 1, HO), start=False,
                                 stop=True).then_inc(s_psum, 1)

            def outputs(b, n):
                k, c = n // DC, n % DC
                pe.wait_ge(p_ready, UN * b + n + 1)
                for i in range(4):
                    h = 4 * c + i
                    last = nc.tensor.matmul(core.bank(6)[:, VW * h:VW * (h + 1)],
                                            pr[:, n % NP, i * P:(i + 1) * P], v1[:, k, h, :],
                                            start=n == 0 and i == 0, stop=k == KT - 1, skip_group_check=True)
                last.then_inc(pv, 1)

            def batch(b):
                pe.wait_ge(ctx_lo, b + 1)
                for n in range(4):
                    c, h = n // 2, n % 2
                    if n < 2:
                        wait_if_positive(pe, v_done, 4 * b)
                    else:
                        pe.wait_ge(k_lo, 4 * b + n - 1)
                    for k in range(DC):
                        last = product3(nc, core.bank(4 + n % 2), [t[:, k, c * P:(c + 1) * P] for t in w2],
                                        [t[:, k, 512 * h:512 * h + 512] for t in c2], k == 0, k == DC - 1)
                    last.then_inc(kv_psum, 1)
                for n in range(4):
                    if n < 2:
                        pe.wait_ge(k_lo, 4 * b + n + 3)
                    else:
                        pe.wait_ge(v_done, 4 * b + n - 1)
                    for i in range(2):
                        kt = 2 * n + i
                        for k in range(DC):
                            last = product3(nc, core.bank(4 + n % 2)[:, D * i:D * i + D],
                                            [t[:, k, kt * P:(kt + 1) * P] for t in c2],
                                            [t[:, k, D:2 * D] for t in w2], k == 0, k == DC - 1)
                    last.then_inc(kv_psum, 1)
                pe.wait_ge(k_lo, 4 * b + 4)
                pe.wait_ge(qd_ready, 4 * b + 4)
                pe.wait_ge(mask_ready, b + 1)
                scores(b, 0)
                scores(b, 1)
                pe.wait_ge(v_done, 4 * b + 4)
                wait_if_positive(pe, o_ready, 2 * b)
                for n in range(UN):
                    if n + 2 < UN:
                        scores(b, n + 2)
                    outputs(b, n)
            each(pe, B, batch)
            pe.wait_ge(o_ready, 2 * B)
            for b in range(B):
                last = nc.tensor.transpose(core.ps[0][:, b * P:(b + 1) * P],
                                           o[:, b, :, :].rearrange("p h d -> p (h d)"), ident[:])
            last.then_inc(oT_psum, 1)
            pe.wait_ge(oT_ready, 1)
            for j in range(TT):
                for h in range(2):
                    last = nc.tensor.matmul(core.bank(2 + j // 2)[:, D * (j % 2):D * (j % 2) + D],
                                            oT[:, h, 2 * j:2 * j + 2, :].rearrange("p b q -> p (b q)"),
                                            wo[:, h, :], start=h == 0, stop=h == 1)
                if j % 2:
                    last.then_inc(y_psum, 1)


def store_x(core, out_d):
    nc = core.nc
    stored = core.sem("stored")
    with nc.Block() as block:
        @block.sync
        def _(sp):
            sp.dma_start(out_d.rearrange("(j p) d -> p j d", p=P), core.x[:]).then_inc(stored, 16)
            sp.wait_ge(stored, 16)


def log1p_coefficients():
    import numpy as np
    z = (np.cos(np.pi * (np.arange(64) + 0.5) / 64) + 1) / 18
    s = np.sqrt(z)
    fit = np.polynomial.chebyshev.Chebyshev.fit(z, 2 * np.arctanh(s) / s, 6, domain=[0, 1 / 9])
    return [float(c) for c in fit.convert(kind=np.polynomial.Polynomial).coef]


def memory0(core, a):
    nc = core.nc
    RANK = D // 4
    TWO_PI = 6.283185307179586
    PI_A, PI_B = 6.28125, 0.0019350051879882812
    PI_C = TWO_PI - PI_A - PI_B
    with ExitStack() as ctx:
        sb = lambda name, shape, dt=F32: core.sb("b_" + name, shape, dt, ctx)
        sem = lambda name: core.sem("b_" + name)
        wB, wC, wout = sb("wB", [P, DC, D]), sb("wC", [P, DC, D]), sb("wout", [P, DC, D])
        wdt1, wdt2 = sb("wdt1", [P, DC, RANK]), sb("wdt2", [RANK, D])
        bB, bC, bdt2, omega = (sb(n, [P, DC]) for n in ("bB", "bC", "bdt2", "omega"))
        bdt1 = sb("bdt1", [RANK, 1])
        bout, skip = sb("bout", [P, D]), sb("skip", [P, D])
        carry = sb("carry", [P, NT])
        t1 = sb("t1", [RANK, NT])
        wide = lambda name: sb(name, [P, DC, NT])
        z, ez, s, s2, poly = wide("z"), wide("ez"), wide("s"), wide("s2"), wide("poly")
        phi, k, sn, cs, half = wide("phi"), wide("k"), wide("sn"), wide("cs"), wide("half")
        content, cr, ci, mr, mi = wide("content"), wide("cr"), wide("ci"), wide("mr"), wide("mi")
        base = sb("base", [P, TT, D])

        w_in, const, pool_step, dve_step = sem("w_in"), sem("const"), sem("pool_step"), sem("dve_step")
        t1_psum, t1_ready, dt_psum = sem("t1_psum"), sem("t1_ready"), sem("dt_psum")
        b_psum, c_psum = sem("b_psum"), sem("c_psum")
        z_ready, ez_abs, ez_ready, r_ready = sem("z_ready"), sem("ez_abs"), sem("ez_ready"), sem("r_ready")
        sn_ready, half_ready = sem("sn_ready"), sem("half_ready")
        ret_ready, y_psum, base_ready, x_out = sem("ret_ready"), sem("y_psum"), sem("base_ready"), sem("x_out")
        norm = Norm(core, "b")
        x, xn, xnT = core.x, core.xn, core.xnT
        flat = lambda v: v[:].rearrange("p c n -> p (c n)")
        block = ctx.enter_context(nc.Block())

        @block.sync
        def _(sp):
            for dst, src in ((wdt1, "W_dt1"), (wB, "W_B"), (wC, "W_C"), (wout, "W_out")):
                sp.dma_start(dst[:], a["L0_attn_" + src].rearrange("(c p) o -> p c o", p=P)).then_inc(w_in, 16)
            sp.dma_start(wdt2[:], a["L0_attn_W_dt2"]).then_inc(w_in, 16)
            for dst, src in ((bB, "b_B"), (bC, "b_C"), (bdt2, "b_dt2"), (omega, "omega_base")):
                sp.dma_start(dst[:], a["L0_attn_" + src]).then_inc(w_in, 16)
            sp.dma_start(bdt1[:], a["L0_attn_b_dt1"]).then_inc(w_in, 16)
            for dst, src in ((bout, "b_out"), (skip, "D")):
                sp.dma_start(dst[:], a["L0_attn_" + src].partition_broadcast(P)).then_inc(w_in, 16)

        WEIGHTS = 16 * 12

        @block.gpsimd
        def _(pool):
            step = stepper(pool, pool_step)
            step(nc.gpsimd.memset(carry[:], 1.0))
            nc.gpsimd.memset(carry[:].rearrange("p (b t) -> p b t", t=T)[:, :, 0:1], 0.0).then_inc(const, 1)
            pool.wait_ge(norm.xn, TT)
            pool.wait_ge(w_in, WEIGHTS)
            step(nc.gpsimd.tensor_tensor(base[:], xn[:], bc(skip[:], 1, TT), ALU.mult))
            step(nc.gpsimd.tensor_tensor(base[:], base[:], bc(bout[:], 1, TT), ALU.add))
            nc.gpsimd.tensor_tensor(base[:], base[:], x[:], ALU.add).then_inc(base_ready, 1)

        @block.scalar
        def _(act):
            norm.scalar(act)
            act.wait_ge(w_in, WEIGHTS)
            act.wait_ge(t1_psum, 1)
            nc.scalar.activation(t1[:], core.bank(2)[0:RANK, :], ACT.Identity, bias=bdt1[:]).then_inc(t1_ready, 1)
            act.wait_ge(z_ready, DC)
            nc.scalar.activation(flat(ez), flat(z), ACT.Abs).then_inc(ez_abs, 1)
            act.wait_ge(ez_abs, 1)
            nc.scalar.activation(flat(ez), flat(ez), ACT.Exp, scale=-1.0).then_inc(ez_ready, 1)
            act.wait_ge(r_ready, 1)
            nc.scalar.activation(flat(sn), flat(phi), ACT.Sin).then_inc(sn_ready, 1)
            nc.scalar.activation(flat(half), flat(phi), ACT.Sin, scale=0.5).then_inc(half_ready, 1)

        @block.vector
        def _(dve):
            step = stepper(dve, dve_step)
            V = nc.vector
            norm.vector(dve, step)
            dve.wait_ge(w_in, WEIGHTS)
            for c in range(DC):
                dve.wait_ge(b_psum, c + 1)
                step(V.scalar_tensor_tensor(content[:, c, :], core.bank(4 + c), bB[:, c:c + 1], xnT[:, c, :],
                                            ALU.add, ALU.mult))
            for c in range(DC):
                dve.wait_ge(dt_psum, c + 1)
                V.tensor_scalar(z[:, c, :], core.bank(c), bdt2[:, c:c + 1], None, ALU.add).then_inc(z_ready, 1)
            dve.wait_ge(ez_ready, 1)
            step(V.tensor_scalar(flat(s), flat(ez), 2.0, None, ALU.add))
            step(V.reciprocal(flat(s), flat(s)))
            step(V.tensor_tensor(flat(s), flat(s), flat(ez), ALU.mult))
            step(V.tensor_tensor(flat(s2), flat(s), flat(s), ALU.mult))
            coef = log1p_coefficients()
            step(V.tensor_scalar(flat(poly), flat(s2), coef[-1], None, ALU.mult))
            for q in coef[-2:0:-1]:
                step(V.scalar_tensor_tensor(flat(poly), flat(poly), q, flat(s2), ALU.add, ALU.mult))
            step(V.scalar_tensor_tensor(flat(poly), flat(poly), coef[0], flat(s), ALU.add, ALU.mult))
            step(V.scalar_tensor_tensor(flat(z), flat(z), 0.0, flat(poly), ALU.max, ALU.add))
            dve.wait_ge(const, 1)
            for c in range(DC):
                step(V.tensor_scalar(z[:, c, :], z[:, c, :], omega[:, c:c + 1], None, ALU.mult))
                step(V.tensor_tensor_scan(phi[:, c, :], carry[:], z[:, c, :], 0.0, ALU.mult, ALU.add))
            step(V.tensor_scalar(flat(k), flat(phi), 1.0 / TWO_PI, MAGIC, ALU.mult, ALU.add))
            step(V.tensor_scalar(flat(k), flat(k), MAGIC, None, ALU.subtract))
            for part in (PI_A, PI_B, PI_C):
                step(V.scalar_tensor_tensor(flat(phi), flat(k), -part, flat(phi), ALU.mult, ALU.add))
            V.tensor_scalar(flat(phi), flat(phi), 3.1415925, -3.1415925, ALU.min, ALU.max).then_inc(r_ready, 1)
            dve.wait_ge(sn_ready, 1)
            step(V.tensor_tensor(flat(ci), flat(content), flat(sn), ALU.mult))
            for c in range(DC):
                step(V.tensor_tensor_scan(mi[:, c, :], carry[:], ci[:, c, :], 0.0, ALU.mult, ALU.add))
            dve.wait_ge(half_ready, 1)
            step(V.scalar_tensor_tensor(flat(cs), flat(half), -2.0, flat(half), ALU.mult, ALU.mult))
            step(V.tensor_scalar(flat(cs), flat(cs), 1.0, None, ALU.add))
            step(V.tensor_tensor(flat(cr), flat(content), flat(cs), ALU.mult))
            for c in range(DC):
                step(V.tensor_tensor_scan(mr[:, c, :], carry[:], cr[:, c, :], 0.0, ALU.mult, ALU.add))
            step(V.tensor_tensor(flat(mi), flat(mi), flat(sn), ALU.mult))
            step(V.tensor_tensor(flat(mr), flat(mr), flat(cs), ALU.mult))
            step(V.tensor_tensor(flat(mr), flat(mr), flat(mi), ALU.add))
            for c in range(DC):
                dve.wait_ge(c_psum, c + 1)
                V.scalar_tensor_tensor(mr[:, c, :], core.bank(6 + c), bC[:, c:c + 1], mr[:, c, :],
                                       ALU.add, ALU.mult).then_inc(ret_ready, 1)
            dve.wait_ge(base_ready, 1)
            for j in range(2):
                dve.wait_ge(y_psum, j + 1)
                V.tensor_tensor(x[:, 2 * j:2 * j + 2, :], base[:, 2 * j:2 * j + 2, :],
                                core.bank(2 + j).rearrange("p (j d) -> p j d", d=D), ALU.add).then_inc(x_out, 1)

        @block.tensor
        def _(pe):
            norm.tensor(pe)
            pe.wait_ge(w_in, WEIGHTS)
            for c in range(DC):
                last = nc.tensor.matmul(core.bank(2)[0:RANK, :], wdt1[:, c, :], xnT[:, c, :], start=c == 0,
                                        stop=c == DC - 1)
            last.then_inc(t1_psum, 1)

            def project(w, first_bank, done):
                for c in range(DC):
                    for i in range(DC):
                        last = nc.tensor.matmul(core.bank(first_bank + c), w[:, i, c * P:(c + 1) * P],
                                                xnT[:, i, :], start=i == 0, stop=i == DC - 1)
                    last.then_inc(done, 1)

            project(wB, 4, b_psum)
            pe.wait_ge(t1_ready, 1)
            for c in range(DC):
                nc.tensor.matmul(core.bank(c), wdt2[:, c * P:(c + 1) * P], t1[:], start=True,
                                 stop=True).then_inc(dt_psum, 1)
            project(wC, 6, c_psum)
            pe.wait_ge(ret_ready, DC)
            for j in range(TT):
                for c in range(DC):
                    last = nc.tensor.matmul(core.bank(2 + j // 2)[:, D * (j % 2):D * (j % 2) + D],
                                            mr[:, c, j * P:(j + 1) * P], wout[:, c, :], start=c == 0,
                                            stop=c == DC - 1)
                if j % 2:
                    last.then_inc(y_psum, 1)


class Gate:

    def __init__(self, core, ctx, tag, top):
        self.c, self.top, self.tag = core, top, tag
        sb = lambda name, shape: core.sb(tag + name, shape, F32, ctx)
        self.rw, self.rb = sb("_gate_w", [P, DC, E]), sb("_gate_b", [P, E])
        self.tri = sb("_gate_tri", [P, E, E])
        self.pick = sb("_gate_pick", [E, E, P])
        self.mx, self.sm = sb("_gate_max", [P, TT]), sb("_gate_sum", [P, TT])
        self.p, self.w = sb("_gate_p", [P, TT, E]), sb("_gate_wt", [P, TT, E])
        self.gt, self.eq = sb("_gate_gt", [P, TT, E, E]), sb("_gate_eq", [P, TT, E, E])
        self.rank = sb("_gate_rank", [P, TT, E])
        self.wT = sb("_gate_wT", [E, NT])
        self.rows = sb("_gate_rows", [P, E, NT])
        sem = lambda name: core.sem(tag + "_gate_" + name)
        self.inn, self.const = sem("in"), sem("const")
        self.logits, self.shifted, self.exp = sem("logits"), sem("shifted"), sem("exp")
        self.weights, self.wT_psum, self.wT_ready = sem("weights"), sem("wT_psum"), sem("wT_ready")
        self.row_psum, self.row_act, self.row_dve = sem("row_psum"), sem("row_act"), sem("row_dve")

    def sync(self, sp, w, b):
        sp.dma_start(self.rw[:], w.rearrange("(c p) e -> p c e", p=P)).then_inc(self.inn, 16)
        sp.dma_start(self.rb[:], b.partition_broadcast(P)).then_inc(self.inn, 16)

    def gpsimd(self, step):
        g = self.c.nc.gpsimd
        step(g.memset(self.tri[:], 1.0))
        g.affine_select(out=self.tri[:], in_=self.tri[:], compare_op=ALU.is_gt, fill=0.0, base=0,
                        pattern=[[1, E], [-1, E]], channel_multiplier=0).then_inc(self.const, 1)
        step(g.memset(self.pick[:], 0.0))
        g.affine_select(out=self.pick[:], in_=self.pick[:], compare_op=ALU.not_equal, fill=1.0, base=0,
                        pattern=[[-1, E], [0, P]], channel_multiplier=1).then_inc(self.const, 1)

    def vector(self, dve, step):
        V = self.c.nc.vector
        p, w = self.p, self.w
        dve.wait_ge(self.const, 2)
        dve.wait_ge(self.inn, 32)
        dve.wait_ge(self.logits, 1)
        lg = self.c.bank(0)[:, 0:TT * E].rearrange("p (j e) -> p j e", e=E)
        step(V.tensor_tensor(p[:], lg, bc(self.rb[:], 1, TT), ALU.add))
        step(V.reduce_max(self.mx[:], p[:], AX))
        V.tensor_tensor(p[:], p[:], bc(self.mx[:], 2, E), ALU.subtract).then_inc(self.shifted, 1)
        dve.wait_ge(self.exp, 1)
        step(V.reduce_sum(self.sm[:], p[:], AX))
        step(V.reciprocal(self.sm[:], self.sm[:]))
        step(V.tensor_tensor(p[:], p[:], bc(self.sm[:], 2, E), ALU.mult))
        mine, other = bc(p[:], 3, E), bc(p[:], 2, E)
        step(V.tensor_tensor(self.gt[:], other, mine, ALU.is_gt))
        step(V.tensor_tensor(self.eq[:], other, mine, ALU.is_equal))
        merged = lambda v: v[:].rearrange("p j e f -> p j (e f)")
        step(V.tensor_tensor(merged(self.eq), merged(self.eq),
                             bc(self.tri[:].rearrange("p e f -> p (e f)"), 1, TT), ALU.mult))
        step(V.tensor_tensor(self.gt[:], self.gt[:], self.eq[:], ALU.add))
        step(V.reduce_sum(self.rank[:], self.gt[:], AX))
        last = V.scalar_tensor_tensor(w[:], self.rank[:], float(self.top), p[:], ALU.is_lt, ALU.mult)
        if self.top > 1:
            step(last)
            step(V.reduce_sum(self.sm[:], w[:], AX))
            step(V.tensor_scalar(self.sm[:], self.sm[:], 1e-8, None, ALU.add))
            step(V.reciprocal(self.sm[:], self.sm[:]))
            last = V.tensor_tensor(w[:], w[:], bc(self.sm[:], 2, E), ALU.mult)
        last.then_inc(self.weights, 1)
        for e in range(1, E, 2):
            dve.wait_ge(self.row_psum, e + 1)
            V.tensor_copy(self.rows[:, e, :], self.c.bank(e % 4)).then_inc(self.row_dve, 1)

    def scalar(self, act):
        A = self.c.nc.scalar
        act.wait_ge(self.shifted, 1)
        A.activation(self.p[:], self.p[:], ACT.Exp).then_inc(self.exp, 1)
        act.wait_ge(self.wT_psum, 1)
        A.copy(self.wT[:], self.c.bank(1)[0:E, :]).then_inc(self.wT_ready, 1)
        for e in range(0, E, 2):
            act.wait_ge(self.row_psum, e + 1)
            A.copy(self.rows[:, e, :], self.c.bank(e % 4)).then_inc(self.row_act, 1)

    def tensor_logits(self, pe, inT):
        t = self.c.nc.tensor
        pe.wait_ge(self.inn, 32)
        for j in range(TT):
            for c in range(DC):
                last = t.matmul(self.c.bank(0)[:, j * E:(j + 1) * E], inT[:, c, j * P:(j + 1) * P],
                                self.rw[:, c, :], start=c == 0, stop=c == DC - 1)
        last.then_inc(self.logits, 1)

    def tensor_rows(self, pe):
        t = self.c.nc.tensor
        pe.wait_ge(self.weights, 1)
        for j in range(TT):
            last = t.transpose(self.c.bank(1)[0:E, j * P:(j + 1) * P], self.w[:, j, :], self.c.ident[:])
        last.then_inc(self.wT_psum, 1)
        pe.wait_ge(self.wT_ready, 1)
        for e in range(E):
            if e >= 4:
                pe.wait_ge(self.row_dve if e % 2 else self.row_act, (e - 4) // 2 + 1)
            t.matmul(self.c.bank(e % 4), self.pick[:, e, :], self.wT[:], start=True,
                     stop=True).then_inc(self.row_psum, 1)


class Experts:

    LAG, RH, RG = 2, 4, 4

    def __init__(self, core, ctx, tag, hidden, func, scale, in_ready, in_count):
        self.c, self.tag, self.func, self.scale = core, tag, func, scale
        self.F, self.NF = hidden, hidden // P
        self.in_ready, self.in_count = in_ready, in_count
        sb = lambda name, shape, dt=F32: core.sb(tag + name, shape, dt, ctx)
        NF, HF = self.NF, self.NF // 2
        self.HF = HF
        self.w1 = [sb(f"_w1_{i}", [P, DC, HF * P]) for i in range(2)]
        self.w2 = [sb(f"_w2_{i}", [P, HF, D]) for i in range(2)]
        self.w1p = [[sb(f"_w1_{i}_{n}", [P, DC, HF * P], F32R) for n in ("hi", "lo")] for i in range(2)]
        self.w2p = [[sb(f"_w2_{i}_{n}", [P, HF, D], F32R) for n in ("hi", "lo")] for i in range(2)]
        self.b1, self.b2 = sb("_b1", [P, E, NF]), sb("_b2", [E, D])
        self.inp = [sb(f"_in_{n}", [P, DC, NT], F32R) for n in ("hi", "lo")]
        self.h, self.g = sb("_h", [P, self.RH, NT]), sb("_g", [P, self.RH, NT])
        self.gp = [sb(f"_g_{n}", [P, self.RG, NT], F32R) for n in ("hi", "lo")]
        sem = lambda name: core.sem(tag + "_" + name)
        self.b_in = sem("b_in")
        self.inn = [sem(f"part{i}_in") for i in range(4)]
        self.hi = [sem(f"part{i}_hi") for i in range(4)]
        self.lo = [sem(f"part{i}_lo") for i in range(4)]
        self.in_hi, self.in_lo = sem("in_hi"), sem("in_lo")
        self.h_psum, self.h_ready, self.g_ready = sem("h_psum"), sem("h_ready"), sem("g_ready")
        self.g_hi, self.g_lo, self.y = sem("g_hi"), sem("g_lo"), sem("y")
        self.x_out = sem("x_out")

    def parts(self):
        return [(self.w1[0], self.w1p[0]), (self.w1[1], self.w1p[1]), (self.w2[0], self.w2p[0]),
                (self.w2[1], self.w2p[1])]

    def sync(self, sp, w1_d, b1_d, w2_d, b2_d):
        HF = self.HF
        rows = HF * P

        def load(e, i):
            one = slice(e, e + 1) if isinstance(e, int) else bass.ds(e, 1)
            if i < 2:
                src = w1_d[one, :, i * rows:(i + 1) * rows].rearrange("o (c p) f -> (o p) c f", p=P)
                dst = self.w1[i]
            else:
                src = w2_d[one, (i - 2) * rows:(i - 1) * rows, :].rearrange("o (f p) d -> (o p) f d", p=P)
                dst = self.w2[i - 2]
            sp.dma_start(dst[:], src).then_inc(self.inn[i], 16)

        load(0, 0)
        sp.dma_start(self.b1[:], b1_d.rearrange("p (e f) -> p e f", e=E)).then_inc(self.b_in, 16)
        sp.dma_start(self.b2[:], b2_d).then_inc(self.b_in, 16)
        for i in range(1, 4):
            load(0, i)
        with sp.Fori(1, E) as e:
            for i in (0, 2, 1, 3):
                sp.wait_ge(self.hi[i], e)
                sp.wait_ge(self.lo[i], e)
                load(e, i)

    def gpsimd(self, pool):
        g = self.c.nc.gpsimd

        def low(e, i):
            raw, (hi, lo) = self.parts()[i]
            pool.wait_ge(self.hi[i], e + 1)
            g.tensor_tensor(lo[:], raw[:], hi[:].bitcast(F32), ALU.subtract).then_inc(self.lo[i], 1)

        def body(e):
            low(e, 1)
            low(e, 3)
            if not isinstance(e, int) or e < E - 1:
                low(e + 1, 0)
                low(e + 1, 2)

        low(0, 0)
        low(0, 2)
        each(pool, E, body)

    def wait_slot(self, engine, sem, e, f, ring):
        wait_if_positive(engine, sem, self.NF * e + f + 1 - ring)

    def scalar(self, act, inT):
        A, NF, HF = self.c.nc.scalar, self.NF, self.HF

        def high(e, i):
            raw, (hi, _) = self.parts()[i]
            act.wait_ge(self.inn[i], 16 * e + 16)
            if not isinstance(e, int) or e > 0:
                act.wait_ge(self.h_psum if i < 2 else self.y, NF * e - (NF - HF if i % 2 == 0 else 0))
            A.copy(hi[:], raw[:]).then_inc(self.hi[i], 1)

        def g_high(e, f):
            act.wait_ge(self.g_ready, NF * e + f + 1)
            self.wait_slot(act, self.y, e, f, self.RG)
            A.copy(self.gp[0][:, f % self.RG, :], self.g[:, f % self.RH, :]).then_inc(self.g_hi, 1)

        def body(e):
            for f in range(NF):
                act.wait_ge(self.h_psum, NF * e + f + 1)
                self.wait_slot(act, self.g_ready, e, f, self.RH)
                bias = self.b1[:, e, f:f + 1] if isinstance(e, int) else self.b1[:, bass.ds(e, 1), f]
                A.activation(self.h[:, f % self.RH, :], self.c.bank(f % 4), self.func,
                             bias=bias).then_inc(self.h_ready, 1)
                if f < 2:
                    high(e, (1, 3)[f])
                if not isinstance(e, int) or e < E - 1:
                    if f == NF - 2:
                        high(e + 1, 0)
                    if f == NF - 1:
                        high(e + 1, 2)
                if f > 0:
                    g_high(e, f - 1)
            g_high(e, NF - 1)

        act.wait_ge(self.in_ready, self.in_count)
        A.copy(self.inp[0][:], inT[:]).then_inc(self.in_hi, 1)
        high(0, 0)
        high(0, 2)
        act.wait_ge(self.b_in, 32)
        each(act, E, body)

    def vector(self, dve, inT, rows):
        V, NF = self.c.nc.vector, self.NF

        def g_low(e, f):
            dve.wait_ge(self.g_hi, NF * e + f + 1)
            V.tensor_tensor(self.gp[1][:, f % self.RG, :], self.g[:, f % self.RH, :],
                            self.gp[0][:, f % self.RG, :].bitcast(F32), ALU.subtract).then_inc(self.g_lo, 1)

        def body(e):
            row = rows[:, e, :] if isinstance(e, int) else rows[:, bass.ds(e, 1), :].rearrange("p o n -> p (o n)")
            for f in range(NF):
                dve.wait_ge(self.h_ready, NF * e + f + 1)
                self.wait_slot(dve, self.g_lo, e, f, self.RH)
                V.tensor_tensor(self.g[:, f % self.RH, :], self.h[:, f % self.RH, :], row,
                                ALU.mult).then_inc(self.g_ready, 1)
                if f > 0:
                    g_low(e, f - 1)
            g_low(e, NF - 1)

        dve.wait_ge(self.in_hi, 1)
        V.tensor_tensor(self.inp[1][:], inT[:], self.inp[0][:].bitcast(F32), ALU.subtract).then_inc(self.in_lo, 1)
        each(dve, E, body)
        dve.wait_ge(self.y, NF * E)
        x = self.c.x
        for i in range(2):
            acc = self.c.ps[2 + i][:].rearrange("p (j w) -> p j w", j=2)[:, :, 0:D]
            V.scalar_tensor_tensor(x[:, 2 * i:2 * i + 2, :], acc, self.scale, x[:, 2 * i:2 * i + 2, :],
                                   ALU.mult, ALU.add).then_inc(self.x_out, 1)

    def tensor(self, pe, wT):
        t, NF, HF = self.c.nc.tensor, self.NF, self.HF

        def first(e, f):
            i = f // HF
            if f % HF == 0:
                pe.wait_ge(self.lo[i], e + 1)
            self.wait_slot(pe, self.h_ready, e, f, 4)
            for k in range(DC):
                last = product3(self.c.nc, self.c.bank(f % 4),
                                [w[:, k, (f % HF) * P:(f % HF + 1) * P] for w in self.w1p[i]],
                                [v[:, k, :] for v in self.inp], k == 0, k == DC - 1)
            last.then_inc(self.h_psum, 1)

        def second(e, f):
            i = f // HF
            if f % HF == 0:
                pe.wait_ge(self.lo[2 + i], e + 1)
            pe.wait_ge(self.g_lo, NF * e + f + 1)
            for j in range(TT):
                last = product3(self.c.nc, self.c.bank(4 + j)[:, 0:D],
                                [g[:, f % self.RG, j * P:(j + 1) * P] for g in self.gp],
                                [w[:, f % HF, :] for w in self.w2p[i]], False, False, skip=True)
            last.then_inc(self.y, 1)

        def body(e):
            for f in range(NF):
                first(e, f)
                if f >= self.LAG:
                    second(e, f - self.LAG)
                elif not isinstance(e, int) or e > 0:
                    second(e - 1, NF + f - self.LAG)

        pe.wait_ge(self.b_in, 32)
        for j in range(TT):
            t.matmul(self.c.bank(4 + j)[:, 0:D], wT[:, j * P:(j + 1) * P], self.b2[:], start=True, stop=False,
                     skip_group_check=True)
        pe.wait_ge(self.in_lo, 1)
        each(pe, E, body)
        for f in range(NF - self.LAG, NF):
            second(E - 1, f)


def ffn0(core, a):
    nc = core.nc
    H, HD = 16, 8
    HP = H // 2
    with ExitStack() as ctx:
        sem = lambda name: core.sem("c_" + name)
        mlaT = core.sb("c_mlaT", [P, DC, NT], F32, ctx)
        mlaT_ready = sem("mlaT_ready")
        norm = Norm(core, "c")
        x, xn, xnT = core.x, core.xn, core.xnT
        with ExitStack() as inner:
            sb = lambda name, shape, dt=F32: core.sb("c_" + name, shape, dt, inner)
            wq, wk, wv = (sb(n, [P, DC, P]) for n in ("wq", "wk", "wv"))
            wo, bo = sb("wo", [P, D]), sb("bo", [P, DC])
            bq, bk, bv = sb("bq", [P, 1]), sb("bk", [P, 1]), sb("bv", [P, P])
            headmask = sb("headmask", [P, H])
            qT, kT = sb("qT", [P, NT]), sb("kT", [P, NT])
            kd = sb("kd", [P, B, H, T])
            vd = sb("vd", [P, B, HP, 2, HD])
            mx, sm = sb("mx", [P, TT, H]), sb("sm", [P, TT, H])
            pr = sb("pr", [P, 2, H, T])
            pT = sb("pT", [P, 2, HP * P])
            ao, aoT = sb("ao", [P, TT, H, HD]), sb("aoT", [P, NT])
            w_in, const, pool_step, dve_step = sem("w_in"), sem("const"), sem("pool_step"), sem("dve_step")
            qk_psum, v_psum, qk_ready, kd_ready, vd_ready = (sem("qk_psum"), sem("v_psum"), sem("qk_ready"),
                                                             sem("kd_ready"), sem("vd_ready"))
            s_psum, s_shifted, p_ready, pT_psum, pT_ready = (sem("s_psum"), sem("s_shifted"), sem("p_ready"),
                                                             sem("pT_psum"), sem("pT_ready"))
            o_psum, o_ready, oT_psum, oT_ready, m_psum = (sem("o_psum"), sem("o_ready"), sem("oT_psum"),
                                                          sem("oT_ready"), sem("m_psum"))
            x_hs = sem("x_hs")
            block = inner.enter_context(nc.Block())

            @block.sync
            def _(sp):
                n = 0
                for dst, src in ((wq, a["L0_ffn_q_w"]), (wk, a["L0_ffn_k_w"]), (wv, a["L0_ffn_v_w"])):
                    sp.dma_start(dst[:], src.rearrange("(c p) o -> p c o", p=P)).then_inc(w_in, 16)
                sp.dma_start(wo[:], a["L0_ffn_o_w"][0:P, :]).then_inc(w_in, 16)
                sp.dma_start(bo[:], a["L0_ffn_o_b"]).then_inc(w_in, 16)
                sp.dma_start(bq[:], a["L0_ffn_q_b"]).then_inc(w_in, 16)
                sp.dma_start(bk[:], a["L0_ffn_k_b"]).then_inc(w_in, 16)
                sp.dma_start(bv[:], a["L0_ffn_v_b"].partition_broadcast(P)).then_inc(w_in, 16)

            WEIGHTS = 16 * 8

            @block.gpsimd
            def _(pool):
                step = stepper(pool, pool_step)
                step(nc.gpsimd.memset(headmask[:], 1.0))
                step(nc.gpsimd.affine_select(out=headmask[:], in_=headmask[:], compare_op=ALU.is_ge, fill=0.0,
                                             base=0, pattern=[[-HD, H]], channel_multiplier=1))
                nc.gpsimd.affine_select(out=headmask[:], in_=headmask[:], compare_op=ALU.is_ge, fill=0.0,
                                        base=HD - 1, pattern=[[HD, H]], channel_multiplier=-1
                                        ).then_inc(const, 1)
                nc.gpsimd.memset(vd[:], 0.0).then_inc(const, 1)
                pool.wait_ge(norm.xn, TT)
                nc.gpsimd.tensor_tensor(x[:], x[:], xn[:], ALU.add).then_inc(x_hs, 1)
                pool.wait_ge(const, 2)
                pool.wait_ge(qk_ready, 2)
                for b in range(1, B, 2):
                    nc.gpsimd.tensor_tensor(kd[:, b, :, :], bc(kT[:, b * T:b * T + T], 1, H),
                                            bc(headmask[:], 2, T), ALU.mult).then_inc(kd_ready, 1)

            @block.scalar
            def _(act):
                norm.scalar(act)
                act.wait_ge(w_in, WEIGHTS)
                for i, (dst, bias) in enumerate(((qT, bq), (kT, bk))):
                    act.wait_ge(qk_psum, i + 1)
                    nc.scalar.activation(dst[:], core.bank(2 + i), ACT.Identity, bias=bias[:]).then_inc(qk_ready, 1)
                for j in range(TT):
                    act.wait_ge(s_shifted, j + 1)
                    nc.scalar.activation(pr[:, j % 2, :, :], pr[:, j % 2, :, :], ACT.Exp,
                                         scale=HD ** -0.5).then_inc(p_ready, 1)
                    act.wait_ge(pT_psum, j + 1)
                    nc.scalar.copy(pT[:, j % 2, :], core.ps[2][:]).then_inc(pT_ready, 1)
                act.wait_ge(oT_psum, 1)
                nc.scalar.copy(aoT[:], core.bank(7)).then_inc(oT_ready, 1)
                for c in range(DC):
                    act.wait_ge(m_psum, c + 1)
                    nc.scalar.activation(mlaT[:, c, :], core.bank(2 + c), ACT.Identity,
                                         bias=bo[:, c:c + 1]).then_inc(mlaT_ready, 1)

            @block.vector
            def _(dve):
                step = stepper(dve, dve_step)
                V = nc.vector
                norm.vector(dve, step)
                dve.wait_ge(w_in, WEIGHTS)
                dve.wait_ge(const, 2)
                dve.wait_ge(v_psum, 1)
                vp = core.ps[2][:].rearrange("p (b h g d) -> p b h g d", b=B, h=HP, g=2)
                bvv = bv[:].rearrange("p (h g d) -> p h g d", h=HP, g=2)
                for g in range(2):
                    half = slice(T * g, T * g + T)
                    for b in range(B):
                        V.tensor_tensor(vd[half, b, :, g, :], vp[half, b, :, g, :], bvv[half, :, g, :],
                                        ALU.add).then_inc(vd_ready, 1)
                dve.wait_ge(qk_ready, 2)
                for b in range(0, B, 2):
                    V.tensor_tensor(kd[:, b, :, :], bc(kT[:, b * T:b * T + T], 1, H), bc(headmask[:], 2, T),
                                    ALU.mult).then_inc(kd_ready, 1)
                for j in range(TT + 1):
                    if j < TT:
                        dve.wait_ge(s_psum, j + 1)
                        sp = core.ps[j % 2][:].rearrange("p (h t) -> p h t", t=T)
                        step(V.reduce_max(mx[:, j, :], sp, AX))
                        if j >= 2:
                            dve.wait_ge(pT_psum, j - 1)
                        V.tensor_tensor(pr[:, j % 2, :, :], sp, bc(mx[:, j, :], 2, T),
                                        ALU.subtract).then_inc(s_shifted, 1)
                    if j >= 1:
                        i = j - 1
                        dve.wait_ge(p_ready, i + 1)
                        step(V.reduce_sum(sm[:, i, :], pr[:, i % 2, :, :], AX))
                        step(V.reciprocal(sm[:, i, :], sm[:, i, :]))
                        dve.wait_ge(o_psum, i + 1)
                        V.tensor_tensor(ao[:, i, :, :], core.bank(6)[:, P * i:P * i + P].rearrange(
                            "p (h d) -> p h d", d=HD), bc(sm[:, i, :], 2, HD), ALU.mult).then_inc(o_ready, 1)

            @block.tensor
            def _(pe):
                t = nc.tensor
                norm.tensor(pe)
                pe.wait_ge(w_in, WEIGHTS)
                for i, w in enumerate((wq, wk)):
                    for c in range(DC):
                        last = t.matmul(core.bank(2 + i), w[:, c, :], xnT[:, c, :], start=c == 0,
                                        stop=c == DC - 1)
                    last.then_inc(qk_psum, 1)
                for b in range(B):
                    for g in range(2):
                        for c in range(DC):
                            last = t.matmul(core.ps[2][T * g:T * g + T, b * P:(b + 1) * P],
                                            xnT[:, c, b * T:b * T + T], wv[:, c, :], start=c == 0,
                                            stop=c == DC - 1)
                last.then_inc(v_psum, 1)

                def scores(j):
                    if j >= 2:
                        pe.wait_ge(s_shifted, j - 1)
                    for g in range(2):
                        b = 2 * j + g
                        for n in range(2):
                            last = t.matmul(core.ps[j % 2][T * g:T * g + T, 512 * n:512 * n + 512],
                                            qT[:, b * T:b * T + T],
                                            kd[:, b, 8 * n:8 * n + 8, :].rearrange("p h t -> p (h t)"),
                                            start=True, stop=True)
                    last.then_inc(s_psum, 1)

                pe.wait_ge(qk_ready, 2)
                pe.wait_ge(kd_ready, B)
                scores(0)
                pe.wait_ge(vd_ready, 2 * B)
                for j in range(TT):
                    if j + 1 < TT:
                        scores(j + 1)
                    pe.wait_ge(p_ready, j + 1)
                    if j >= 1:
                        pe.wait_ge(pT_ready, j)
                    for h in range(HP):
                        last = t.transpose(core.ps[2][:, h * P:(h + 1) * P],
                                           pr[:, j % 2, 2 * h:2 * h + 2, :].rearrange("p h t -> p (h t)"),
                                           core.ident[:])
                    last.then_inc(pT_psum, 1)
                    pe.wait_ge(pT_ready, j + 1)
                    if j >= 1:
                        pe.wait_ge(o_ready, j)
                    for g in range(2):
                        for h in range(HP):
                            last = t.matmul(core.bank(6)[T * g:T * g + T, P * j + 16 * h:P * j + 16 * h + 16],
                                            pT[:, j % 2, h * P + T * g:h * P + T * g + T],
                                            vd[:, 2 * j + g, h, :, :].rearrange("p g d -> p (g d)"),
                                            start=True, stop=True)
                    last.then_inc(o_psum, 1)
                pe.wait_ge(o_ready, TT)
                for j in range(TT):
                    last = t.transpose(core.bank(7)[:, j * P:(j + 1) * P],
                                       ao[:, j, :, :].rearrange("p h d -> p (h d)"), core.ident[:])
                last.then_inc(oT_psum, 1)
                pe.wait_ge(oT_ready, 1)
                for c in range(DC):
                    t.matmul(core.bank(2 + c), wo[:, c * P:(c + 1) * P], aoT[:], start=True,
                             stop=True).then_inc(m_psum, 1)
        moe(core, ctx, "d", 2, 4 * P, ACT.Gelu, 0.3, mlaT, mlaT_ready, a["L0_ffn_router_w"],
            a["L0_ffn_router_b"], a["L0_ffn_w1"], a["L0_ffn_b1"], a["L0_ffn_w2"], a["L0_ffn_b2"], None)


def moe(core, ctx, tag, top, hidden, func, scale, inT, in_ready, rw, rb, w1, b1, w2, b2, norm):
    nc = core.nc
    gate = Gate(core, ctx, tag, top)
    experts = Experts(core, ctx, tag, hidden, func, scale, in_ready, DC)
    pool_step, dve_step = core.sem(tag + "_pool_step"), core.sem(tag + "_dve_step")
    block = ctx.enter_context(nc.Block())

    @block.sync
    def _(sp):
        gate.sync(sp, rw, rb)
        experts.sync(sp, w1, b1, w2, b2)

    @block.gpsimd
    def _(pool):
        gate.gpsimd(stepper(pool, pool_step))
        experts.gpsimd(pool)

    @block.scalar
    def _(act):
        if norm:
            norm.scalar(act)
        gate.scalar(act)
        experts.scalar(act, inT)

    @block.vector
    def _(dve):
        step = stepper(dve, dve_step)
        if norm:
            norm.vector(dve, step)
        gate.vector(dve, step)
        experts.vector(dve, inT, gate.rows)

    @block.tensor
    def _(pe):
        if norm:
            norm.tensor(pe)
        gate.tensor_logits(pe, inT)
        gate.tensor_rows(pe)
        pe.wait_ge(gate.row_act, E // 2)
        pe.wait_ge(gate.row_dve, E // 2)
        experts.tensor(pe, gate.wT)


def xattn1(core, a):
    nc = core.nc
    H, HD = 16, 64
    HP = H // 2
    NG = HP // 2
    x, xn, xnT = core.x, core.xn, core.xnT
    with ExitStack() as ctx:
        qc = core.sb("e_qc", [P, DC, B, H * T], F32, ctx)
        norm = Norm(core, "e")

        with ExitStack() as inner:
            sb = lambda name, shape, dt=F32: core.sb("e_" + name, shape, dt, inner)
            sem = lambda name: core.sem("e_" + name)
            wq, wk = sb("wq", [P, DC, H * HD]), sb("wk", [P, HP, D])
            wk2 = [sb("wk_" + n, [P, HP, D], F32R) for n in ("hi", "lo")]
            q2 = [sb("q_" + n, [P, HP, NT], F32R) for n in ("hi", "lo")]
            w_in, wk_hi, wk_lo = sem("w_in"), sem("wk_hi"), sem("wk_lo")
            q_psum, q_hi, q_lo = sem("q_psum"), sem("q_hi"), sem("q_lo")
            c_psum, c_act, c_dve, dve_step = sem("c_psum"), sem("c_act"), sem("c_dve"), sem("dve_step")
            block = inner.enter_context(nc.Block())
            NB = 4

            @block.sync
            def _(sp):
                sp.dma_start(wk[:], a["L1_xattn_w_k"].rearrange("(p r) d -> r p d", r=P)).then_inc(w_in, 16)
                sp.dma_start(wq[:], a["L1_xattn_w_q"].rearrange("(c p) o -> p c o", p=P)).then_inc(w_in, 16)

            @block.gpsimd
            def _(pool):
                pool.wait_ge(wk_hi, 1)
                nc.gpsimd.tensor_tensor(wk2[1][:], wk[:], wk2[0][:].bitcast(F32), ALU.subtract).then_inc(wk_lo, 1)

            def into(u):
                h, c = u // DC, u % DC
                return qc[:, c, :, h * T:(h + 1) * T]

            @block.scalar
            def _(act):
                norm.scalar(act)
                act.wait_ge(w_in, 32)
                nc.scalar.copy(wk2[0][:], wk[:]).then_inc(wk_hi, 1)
                for p in range(HP):
                    act.wait_ge(q_psum, p + 1)
                    nc.scalar.copy(q2[0][:, p, :], core.bank(2 + p % 2)).then_inc(q_hi, 1)
                for u in range(0, H * DC, 2):
                    act.wait_ge(c_psum, u + 1)
                    nc.scalar.mul(into(u), core.bank(4 + u % NB).rearrange("p (b q) -> p b q", b=B),
                                  HD ** -0.5).then_inc(c_act, 1)

            @block.vector
            def _(dve):
                norm.vector(dve, stepper(dve, dve_step))
                for p in range(HP):
                    dve.wait_ge(q_hi, p + 1)
                    nc.vector.tensor_tensor(q2[1][:, p, :], core.bank(2 + p % 2), q2[0][:, p, :].bitcast(F32),
                                            ALU.subtract).then_inc(q_lo, 1)
                for u in range(1, H * DC, 2):
                    dve.wait_ge(c_psum, u + 1)
                    nc.vector.tensor_scalar(into(u), core.bank(4 + u % NB).rearrange("p (b q) -> p b q", b=B),
                                            HD ** -0.5, None, ALU.mult).then_inc(c_dve, 1)

            @block.tensor
            def _(pe):
                norm.tensor(pe)
                pe.wait_ge(w_in, 32)
                for p in range(HP):
                    if p >= 2:
                        pe.wait_ge(q_lo, p - 1)
                    for c in range(DC):
                        last = nc.tensor.matmul(core.bank(2 + p % 2), wq[:, c, p * P:(p + 1) * P], xnT[:, c, :],
                                                start=c == 0, stop=c == DC - 1)
                    last.then_inc(q_psum, 1)
                pe.wait_ge(wk_lo, 1)
                for u in range(H * DC):
                    h, c = u // DC, u % DC
                    pe.wait_ge(q_lo, h // 2 + 1)
                    if u >= NB:
                        pe.wait_ge(c_dve if u % 2 else c_act, (u - NB) // 2 + 1)
                    rows = slice(HD * (h % 2), HD * (h % 2) + HD)
                    product3(nc, core.bank(4 + u % NB), [w[rows, h // 2, c * P:(c + 1) * P] for w in wk2],
                             [q[rows, h // 2, :] for q in q2], True, True).then_inc(c_psum, 1)

        with ExitStack() as inner:
            sb = lambda name, shape, dt=F32: core.sb("f_" + name, shape, dt, inner)
            sem = lambda name: core.sem("f_" + name)
            NPR = 2
            rawT, raw = sb("rawT", [P, DC, S]), sb("raw", [P, KT, D])
            cT = [sb("cT_" + n, [P, DC, S], F32R) for n in ("hi", "lo")]
            cN = [sb("cN_" + n, [P, KT, D], F32R) for n in ("hi", "lo")]
            qb = [sb("qb_" + n, [P, DC, H * T], F32R) for n in ("hi", "lo")]
            pr = sb("pr", [P, NPR, S])
            pT = [sb("pT_" + n, [P, 2, KT, 2 * P], F32R) for n in ("hi", "lo")]
            negmax, total = sb("negmax", [P, HP]), sb("total", [P, HP])
            t_in, n_in = sem("t_in"), sem("n_in")
            t_hi, t_lo, n_hi, n_lo, qb_hi, qb_lo = (sem("t_hi"), sem("t_lo"), sem("n_hi"), sem("n_lo"),
                                                    sem("qb_hi"), sem("qb_lo"))
            s_psum, max_ready, exp_ready, recip, p_ready = (sem("s_psum"), sem("max_ready"), sem("exp_ready"),
                                                            sem("recip"), sem("p_ready"))
            pT_psum, pT_hi, pT_lo, o_psum, o_read = (sem("pT_psum"), sem("pT_hi"), sem("pT_lo"), sem("o_psum"),
                                                     sem("o_read"))
            block = inner.enter_context(nc.Block())

            def one(v, b):
                return v[b, :, :] if isinstance(b, int) else v[bass.ds(b, 1), :, :].rearrange("o p f -> (o p) f")

            @block.sync
            def _(sp):
                def load(b):
                    sp.dma_start(rawT[:], one(a["ctxT"], b).rearrange("(c p) k -> p c k", p=P)).then_inc(t_in, 16)
                    sp.dma_start(raw[:], one(a["ctx"], b).rearrange("(k p) d -> p k d", p=P)).then_inc(n_in, 16)

                load(0)
                with sp.Fori(1, B) as b:
                    sp.wait_ge(t_lo, b)
                    sp.wait_ge(n_lo, b)
                    load(b)

            @block.gpsimd
            def _(pool):
                def split(b):
                    pool.wait_ge(t_hi, b + 1)
                    nc.gpsimd.tensor_tensor(cT[1][:], rawT[:], cT[0][:].bitcast(F32),
                                            ALU.subtract).then_inc(t_lo, 1)
                    pool.wait_ge(n_hi, b + 1)
                    nc.gpsimd.tensor_tensor(cN[1][:], raw[:], cN[0][:].bitcast(F32),
                                            ALU.subtract).then_inc(n_lo, 1)

                each(pool, B, split)

            @block.scalar
            def _(act):
                def before(b):
                    act.wait_ge(t_in, 16 * b + 16)
                    wait_if_positive(act, s_psum, HP * b)
                    nc.scalar.copy(cT[0][:], rawT[:]).then_inc(t_hi, 1)
                    src = qc[:, :, b, :] if isinstance(b, int) else \
                        qc[:, :, bass.ds(b, 1), :].rearrange("p c o n -> p c (o n)")
                    nc.scalar.copy(qb[0][:], src).then_inc(qb_hi, 1)

                def context(b):
                    act.wait_ge(n_in, 16 * b + 16)
                    wait_if_positive(act, o_psum, NG * b)
                    nc.scalar.copy(cN[0][:], raw[:]).then_inc(n_hi, 1)

                def high(b, p):
                    act.wait_ge(pT_psum, HP * b + p + 1)
                    if p % 2 == 0:
                        wait_if_positive(act, o_psum, NG * b + p // 2 - 1)
                    g = (p // 2) % 2
                    nc.scalar.copy(pT[0][:, g, :, P * (p % 2):P * (p % 2) + P],
                                   core.ps[2][:].rearrange("p (k n) -> p k n", n=P)).then_inc(pT_hi, 1)

                def outputs(b, g):
                    act.wait_ge(o_psum, NG * b + g + 1)
                    dst = qc[:, :, b, 2 * P * g:2 * P * g + 2 * P] if isinstance(b, int) else \
                        qc[:, :, bass.ds(b, 1), 2 * P * g:2 * P * g + 2 * P].rearrange("p c o n -> p c (o n)")
                    nc.scalar.copy(dst, core.bank(6 + g % 2).rearrange("p (c n) -> p c n", c=DC)
                                   ).then_inc(o_read, 1)

                def batch(b):
                    for p in range(HP):
                        act.wait_ge(max_ready, HP * b + p + 1)
                        wait_if_positive(act, pT_psum, HP * b + p + 1 - NPR)
                        nc.scalar.activation(pr[:, p % NPR, :], core.ps[p % 2][:], ACT.Exp,
                                             bias=negmax[:, p:p + 1], accum_out=total[:, p:p + 1]
                                             ).then_inc(exp_ready, 1)
                        if p == 0:
                            context(b)
                        if p > 0:
                            high(b, p - 1)
                        if p >= 4 and p % 2 == 0:
                            outputs(b, p // 2 - 2)
                    if not isinstance(b, int) or b < B - 1:
                        before(b + 1)
                    high(b, HP - 1)
                    outputs(b, NG - 2)
                    outputs(b, NG - 1)

                before(0)
                each(act, B, batch)

            @block.vector
            def _(dve):
                def before(b):
                    dve.wait_ge(qb_hi, b + 1)
                    src = qc[:, :, b, :] if isinstance(b, int) else \
                        qc[:, :, bass.ds(b, 1), :].rearrange("p c o n -> p c (o n)")
                    nc.vector.tensor_tensor(qb[1][:], src, qb[0][:].bitcast(F32), ALU.subtract).then_inc(qb_lo, 1)

                def low(b, p):
                    dve.wait_ge(pT_hi, HP * b + p + 1)
                    g = (p // 2) % 2
                    cols = slice(P * (p % 2), P * (p % 2) + P)
                    nc.vector.tensor_tensor(pT[1][:, g, :, cols], core.ps[2][:].rearrange("p (k n) -> p k n", n=P),
                                            pT[0][:, g, :, cols].bitcast(F32), ALU.subtract).then_inc(pT_lo, 1)

                def batch(b):
                    for p in range(HP):
                        n = HP * b + p
                        dve.wait_ge(s_psum, n + 1)
                        nc.vector.tensor_reduce(negmax[:, p:p + 1], core.ps[p % 2][:], AX, ALU.max,
                                                negate=True).then_inc(max_ready, 1)
                        dve.wait_ge(exp_ready, n + 1)
                        nc.vector.reciprocal(total[:, p:p + 1], total[:, p:p + 1]).then_inc(recip, 1)
                        dve.wait_ge(recip, n + 1)
                        nc.vector.tensor_scalar(pr[:, p % NPR, :], pr[:, p % NPR, :], total[:, p:p + 1], None,
                                                ALU.mult).then_inc(p_ready, 1)
                        if p > 0:
                            low(b, p - 1)
                    if not isinstance(b, int) or b < B - 1:
                        before(b + 1)
                    low(b, HP - 1)

                before(0)
                each(dve, B, batch)

            @block.tensor
            def _(pe):
                def scores(b, p):
                    wait_if_positive(pe, exp_ready, HP * b + p - 1)
                    for h in range(2):
                        for c in range(DC):
                            last = product3(nc, core.bank(2 * (p % 2) + h),
                                            [q[:, c, p * P:(p + 1) * P] for q in qb],
                                            [t[:, c, 512 * h:512 * h + 512] for t in cT], c == 0, c == DC - 1)
                    last.then_inc(s_psum, 1)

                def transposes(b, p):
                    pe.wait_ge(p_ready, HP * b + p + 1)
                    wait_if_positive(pe, pT_lo, HP * b + p)
                    for k in range(KT):
                        last = nc.tensor.transpose(core.ps[2][:, k * P:(k + 1) * P],
                                                   pr[:, p % NPR, k * P:(k + 1) * P], core.ident[:])
                    last.then_inc(pT_psum, 1)

                def outputs(b, g):
                    pe.wait_ge(pT_lo, HP * b + 2 * g + 2)
                    wait_if_positive(pe, o_read, NG * b + g - 1)
                    for c in range(DC):
                        for k in range(KT):
                            last = product3(nc, core.bank(6 + g % 2)[:, 2 * P * c:2 * P * c + 2 * P],
                                            [t[:, k, c * P:(c + 1) * P] for t in cN],
                                            [t[:, g % 2, k, :] for t in pT], k == 0, k == KT - 1)
                    last.then_inc(o_psum, 1)

                def batch(b):
                    pe.wait_ge(t_lo, b + 1)
                    pe.wait_ge(qb_lo, b + 1)
                    scores(b, 0)
                    scores(b, 1)
                    for p in range(HP):
                        transposes(b, p)
                        if p + 2 < HP:
                            scores(b, p + 2)
                        if p == 2:
                            pe.wait_ge(n_lo, b + 1)
                        if p >= 2 and p % 2 == 0:
                            outputs(b, p // 2 - 1)
                    outputs(b, NG - 1)

                each(pe, B, batch)

        with ExitStack() as inner:
            sb = lambda name, shape, dt=F32: core.sb("g_" + name, shape, dt, inner)
            sem = lambda name: core.sem("g_" + name)
            wv, wo = sb("wv", [P, DC, H * HD]), sb("wo", [P, HP, D])
            oT = sb("oT", [P, HP, NT])
            w_in, v_psum, oT_act, oT_dve, y_psum, x_out = (sem("w_in"), sem("v_psum"), sem("oT_act"),
                                                           sem("oT_dve"), sem("y_psum"), sem("x_out"))
            block = inner.enter_context(nc.Block())

            @block.sync
            def _(sp):
                sp.dma_start(wv[:], a["L1_xattn_w_v"].rearrange("(c p) o -> p c o", p=P)).then_inc(w_in, 16)
                sp.dma_start(wo[:], a["L1_xattn_w_o"].rearrange("(h p) o -> p h o", p=P)).then_inc(w_in, 16)

            @block.scalar
            def _(act):
                for p in range(0, HP, 2):
                    act.wait_ge(v_psum, p + 1)
                    nc.scalar.copy(oT[:, p, :], core.bank(p % 4)).then_inc(oT_act, 1)

            @block.vector
            def _(dve):
                for p in range(1, HP, 2):
                    dve.wait_ge(v_psum, p + 1)
                    nc.vector.tensor_copy(oT[:, p, :], core.bank(p % 4)).then_inc(oT_dve, 1)
                for j in range(2):
                    dve.wait_ge(y_psum, j + 1)
                    nc.vector.tensor_tensor(x[:, 2 * j:2 * j + 2, :], x[:, 2 * j:2 * j + 2, :],
                                            core.bank(4 + j).rearrange("p (j d) -> p j d", d=D),
                                            ALU.add).then_inc(x_out, 1)

            @block.tensor
            def _(pe):
                pe.wait_ge(w_in, 32)
                for p in range(HP):
                    if p >= 4:
                        pe.wait_ge(oT_dve if p % 2 else oT_act, (p - 4) // 2 + 1)
                    for g in range(2):
                        h = 2 * p + g
                        for c in range(DC):
                            last = nc.tensor.matmul(core.bank(p % 4)[HD * g:HD * g + HD, :],
                                                    wv[:, c, h * HD:(h + 1) * HD],
                                                    qc[:, c, :, h * T:(h + 1) * T], start=c == 0,
                                                    stop=c == DC - 1)
                    last.then_inc(v_psum, 1)
                pe.wait_ge(oT_act, HP // 2)
                pe.wait_ge(oT_dve, HP // 2)
                for j in range(TT):
                    for p in range(HP):
                        last = nc.tensor.matmul(core.bank(4 + j // 2)[:, D * (j % 2):D * (j % 2) + D],
                                                oT[:, p, j * P:(j + 1) * P], wo[:, p, :], start=p == 0,
                                                stop=p == HP - 1)
                    if j % 2:
                        last.then_inc(y_psum, 1)


def attn1(core, a):
    nc = core.nc
    H, HD = 8, 64
    HC = H * HD // P
    EPS = 1e-6
    x, xn, xnT = core.x, core.xn, core.xnT
    with ExitStack() as ctx:
        sb = lambda name, shape, dt=F32: core.sb("h_" + name, shape, dt, ctx)
        sem = lambda name: core.sem("h_" + name)
        wq, wk, wv = (sb(n, [P, DC, H * HD]) for n in ("wq", "wk", "wv"))
        wo = sb("wo", [P, HC, D])
        bq, bk, bv, alpha, aug = (sb(n, [P, HC]) for n in ("bq", "bk", "bv", "alpha", "aug"))
        decay, rest = sb("decay", [P, HC]), sb("rest", [P, HC])
        bo, lns, lnb = (sb(n, [P, D]) for n in ("bo", "lns", "lnb"))
        carry = sb("carry", [P, NT])
        dcarry = sb("dcarry", [P, HC, NT])
        sel = sb("sel", [P, HC, H])
        selT = sb("selT", [H, HC, P])
        wide = lambda name: sb(name, [P, HC, NT])
        q, prod, v, u, st, sig = wide("q"), wide("prod"), wide("v"), wide("u"), wide("st"), wide("sig")
        at, mx, sm = sb("at", [P, TT, H]), sb("mx", [P, TT]), sb("sm", [P, TT])
        atT = sb("atT", [H, NT])
        y = sb("y", [P, TT, D])
        w_in, const, pool_step, dve_step = sem("w_in"), sem("const"), sem("pool_step"), sem("dve_step")
        q_psum, k_psum, v_psum = sem("q_psum"), sem("k_psum"), sem("v_psum")
        decay_ready, q_ready, prod_ready, v_ready, sig_ready = (sem("decay_ready"), sem("q_ready"),
                                                                sem("prod_ready"), sem("v_ready"),
                                                                sem("sig_ready"))
        s_psum, shifted, exp_ready, at_ready = sem("s_psum"), sem("shifted"), sem("exp_ready"), sem("at_ready")
        atT_psum, atT_ready, row_psum, o_ready = (sem("atT_psum"), sem("atT_ready"), sem("row_psum"),
                                                  sem("o_ready"))
        y_psum, out_ready, x_out, rest_ready = sem("y_psum"), sem("out_ready"), sem("x_out"), sem("rest_ready")
        norm, norm2 = Norm(core, "h"), Norm(core, "i")
        block = ctx.enter_context(nc.Block())

        @block.sync
        def _(sp):
            for dst, src in ((wq, "Wq"), (wk, "Wk"), (wv, "Wv"), (wo, "Wo")):
                sp.dma_start(dst[:], a["L1_attn_" + src].rearrange("(c p) o -> p c o", p=P)).then_inc(w_in, 16)
            for dst, src in ((bq, "bq"), (bk, "bk"), (bv, "bv"), (alpha, "alpha"), (aug, "aug_param")):
                sp.dma_start(dst[:], a["L1_attn_" + src]).then_inc(w_in, 16)
            for dst, src in ((bo, "bo"), (lns, "ln_scale"), (lnb, "ln_bias")):
                sp.dma_start(dst[:], a["L1_attn_" + src].partition_broadcast(P)).then_inc(w_in, 16)

        WEIGHTS = 16 * 12

        @block.gpsimd
        def _(pool):
            g = nc.gpsimd
            step = stepper(pool, pool_step)
            step(g.memset(carry[:], 1.0))
            g.memset(carry[:].rearrange("p (b t) -> p b t", t=T)[:, :, 0:1], 0.0).then_inc(const, 1)
            step(g.memset(sel[:], 1.0))
            step(g.affine_select(out=sel[:], in_=sel[:], compare_op=ALU.is_ge, fill=0.0, base=0,
                                 pattern=[[2 * HD, HC], [-HD, H]], channel_multiplier=1))
            g.affine_select(out=sel[:], in_=sel[:], compare_op=ALU.is_ge, fill=0.0, base=HD - 1,
                            pattern=[[-2 * HD, HC], [HD, H]], channel_multiplier=-1).then_inc(const, 1)
            step(g.memset(selT[:], 1.0))
            step(g.affine_select(out=selT[:], in_=selT[:], compare_op=ALU.is_ge, fill=0.0, base=0,
                                 pattern=[[2 * HD, HC], [1, P]], channel_multiplier=-HD))
            g.affine_select(out=selT[:], in_=selT[:], compare_op=ALU.is_ge, fill=0.0, base=HD - 1,
                            pattern=[[-2 * HD, HC], [-1, P]], channel_multiplier=HD).then_inc(const, 1)
            pool.wait_ge(decay_ready, 1)
            pool.wait_ge(const, 1)
            for c in range(HC):
                g.tensor_scalar(dcarry[:, c, :], carry[:], decay[:, c:c + 1], None,
                                ALU.mult).then_inc(rest_ready, 1)

        @block.scalar
        def _(act):
            A = nc.scalar
            norm.scalar(act)
            act.wait_ge(w_in, WEIGHTS)
            A.activation(decay[:], alpha[:], ACT.Sigmoid).then_inc(decay_ready, 1)
            for c in range(HC):
                act.wait_ge(q_psum, c + 1)
                A.activation(q[:, c, :], core.bank(2 + c % 2), ACT.Identity, bias=bq[:, c:c + 1]).then_inc(q_ready, 1)
            for c in range(HC):
                act.wait_ge(q_ready, c + 1)
                A.activation(sig[:, c, :], q[:, c, :], ACT.Sigmoid, scale=aug[:, c:c + 1]).then_inc(sig_ready, 1)
            for c in range(HC):
                act.wait_ge(v_psum, c + 1)
                A.activation(v[:, c, :], core.bank(6 + c % 2), ACT.Identity, bias=bv[:, c:c + 1]).then_inc(v_ready, 1)
            act.wait_ge(shifted, 1)
            A.activation(at[:], at[:], ACT.Exp, scale=HD ** -0.5).then_inc(exp_ready, 1)
            act.wait_ge(atT_psum, 1)
            A.copy(atT[:], core.bank(1)[0:H, :]).then_inc(atT_ready, 1)
            norm2.scalar_std(act)

        @block.vector
        def _(dve):
            V = nc.vector
            step = stepper(dve, dve_step)
            norm.vector(dve, step)
            dve.wait_ge(w_in, WEIGHTS)
            dve.wait_ge(decay_ready, 1)
            step(V.tensor_scalar(rest[:], decay[:], -1.0, 1.0, ALU.mult, ALU.add))
            for c in range(HC):
                dve.wait_ge(k_psum, c + 1)
                dve.wait_ge(q_ready, c + 1)
                V.scalar_tensor_tensor(prod[:, c, :], core.bank(4 + c % 2), bk[:, c:c + 1], q[:, c, :],
                                       ALU.add, ALU.mult).then_inc(prod_ready, 1)
            dve.wait_ge(s_psum, 1)
            lg = core.bank(0)[:, 0:TT * H].rearrange("p (j h) -> p j h", h=H)
            step(V.reduce_max(mx[:], lg, AX))
            V.tensor_tensor(at[:], lg, bc(mx[:], 2, H), ALU.subtract).then_inc(shifted, 1)
            dve.wait_ge(exp_ready, 1)
            step(V.reduce_sum(sm[:], at[:], AX))
            step(V.reciprocal(sm[:], sm[:]))
            V.tensor_tensor(at[:], at[:], bc(sm[:], 2, H), ALU.mult).then_inc(at_ready, 1)
            dve.wait_ge(rest_ready, HC)
            dve.wait_ge(v_ready, HC)
            dve.wait_ge(sig_ready, HC)
            for c in range(HC):
                dve.wait_ge(row_psum, c + 1)
                step(V.scalar_tensor_tensor(u[:, c, :], core.bank(2 + c), rest[:, c:c + 1], v[:, c, :],
                                            ALU.mult, ALU.mult))
                step(V.tensor_tensor_scan(st[:, c, :], dcarry[:, c, :], u[:, c, :], 0.0, ALU.mult, ALU.add))
                step(V.tensor_tensor(u[:, c, :], st[:, c, :], q[:, c, :], ALU.mult))
                V.tensor_tensor(prod[:, c, :], u[:, c, :], sig[:, c, :], ALU.add).then_inc(o_ready, 1)
            for j in range(2):
                dve.wait_ge(y_psum, j + 1)
                step(V.tensor_tensor(y[:, 2 * j:2 * j + 2, :], core.bank(6 + j).rearrange("p (j d) -> p j d", d=D),
                                     bc(bo[:], 1, 2), ALU.add))
            norm2.vector_norm(dve, step, y, y, EPS, out_ready)
            dve.wait_ge(out_ready, TT)
            step(V.tensor_tensor(y[:], y[:], bc(lns[:], 1, TT), ALU.mult))
            step(V.tensor_tensor(y[:], y[:], bc(lnb[:], 1, TT), ALU.add))
            V.tensor_tensor(x[:], x[:], y[:], ALU.add).then_inc(x_out, 1)

        @block.tensor
        def _(pe):
            t = nc.tensor
            norm.tensor(pe)
            pe.wait_ge(w_in, WEIGHTS)

            def project(w, first_bank, done, read):
                for c in range(HC):
                    if c >= 2:
                        pe.wait_ge(read, c - 1)
                    for i in range(DC):
                        last = t.matmul(core.bank(first_bank + c % 2), w[:, i, c * P:(c + 1) * P], xnT[:, i, :],
                                        start=i == 0, stop=i == DC - 1)
                    last.then_inc(done, 1)

            project(wq, 2, q_psum, q_ready)
            project(wk, 4, k_psum, prod_ready)
            project(wv, 6, v_psum, v_ready)
            pe.wait_ge(const, 3)
            pe.wait_ge(prod_ready, HC)
            for j in range(TT):
                for c in range(HC):
                    last = t.matmul(core.bank(0)[:, j * H:(j + 1) * H], prod[:, c, j * P:(j + 1) * P], sel[:, c, :],
                                    start=c == 0, stop=c == HC - 1)
            last.then_inc(s_psum, 1)
            pe.wait_ge(at_ready, 1)
            for j in range(TT):
                last = t.transpose(core.bank(1)[0:H, j * P:(j + 1) * P], at[:, j, :], core.ident[:])
            last.then_inc(atT_psum, 1)
            pe.wait_ge(atT_ready, 1)
            for c in range(HC):
                t.matmul(core.bank(2 + c), selT[:, c, :], atT[:], start=True, stop=True).then_inc(row_psum, 1)
            pe.wait_ge(v_ready, HC)
            pe.wait_ge(o_ready, HC)
            for j in range(TT):
                for c in range(HC):
                    last = t.matmul(core.bank(6 + j // 2)[:, D * (j % 2):D * (j % 2) + D],
                                    prod[:, c, j * P:(j + 1) * P], wo[:, c, :], start=c == 0, stop=c == HC - 1)
                if j % 2:
                    last.then_inc(y_psum, 1)


def ffn1(core, a):
    with ExitStack() as ctx:
        norm = Norm(core, "j")
        moe(core, ctx, "k", 1, 8 * P, ACT.Silu, 1.0, core.xnT, norm.xnT, a["L1_ffn_Wg"], a["L1_ffn_bg"],
            a["L1_ffn_W1"], a["L1_ffn_b1"], a["L1_ffn_W2"], a["L1_ffn_b2"], norm)


def program(nc, a, out):
    with ExitStack() as ctx:
        core = Core(nc, ctx)
        xattn0(core, a["x"], a["ctxT"], a["maskT"], a["L0_xattn_Wq"], a["L0_xattn_Wkv"], a["L0_xattn_Wo"],
               a["L0_xattn_nbias"])
        memory0(core, a)
        ffn0(core, a)
        core.clear_sems()
        xattn1(core, a)
        attn1(core, a)
        ffn1(core, a)
        store_x(core, out)


def layout(inputs):
    import numpy as np

    a = {k: np.asarray(v) for k, v in inputs.items()}
    ctx, mask = a.pop("ctx_1024"), a.pop("mask_BxSxS2_bk0")
    a["x"] = a["x"].reshape(NT, D)
    a["ctx"], a["ctxT"] = ctx, ctx.transpose(0, 2, 1)
    a["maskT"] = mask.reshape(B, T, KT, P).transpose(0, 3, 2, 1).reshape(B, P, KT * T)
    for n in ("Wq", "Wkv"):
        a["L0_xattn_" + n] = a["L0_xattn_" + n].T
    a["L0_xattn_Wo"] = a["L0_xattn_Wo"].T.reshape(8, 2, 16, D).transpose(1, 0, 2, 3).reshape(D, D)
    a["L0_ffn_q_w"] = a["L0_ffn_q_w"].reshape(D, 16, 2, 8)[:, :, 0, :].reshape(D, P)
    a["L0_ffn_q_b"] = a["L0_ffn_q_b"].reshape(16, 2, 8)[:, 0, :].reshape(P)
    a["L1_xattn_w_k"] = a["L1_xattn_w_k"].T
    for n in ("L0_attn_b_B", "L0_attn_b_C", "L0_attn_b_dt2", "L0_attn_omega_base", "L0_ffn_o_b", "L0_ffn_q_b",
              "L0_ffn_k_b", "L0_ffn_b1", "L1_ffn_b1", "L1_attn_bq", "L1_attn_bk", "L1_attn_bv",
              "L1_attn_alpha", "L1_attn_aug_param"):
        a[n] = a[n].reshape(-1, P).T
    a["L0_attn_b_dt1"] = a["L0_attn_b_dt1"].reshape(-1, 1)
    return {k: np.ascontiguousarray(v) for k, v in a.items()}


def kernel(**inputs):
    import concourse.bacc as bacc
    from concourse.bass_utils import run_bass_kernel_spmd

    nc = bacc.Bacc("TRN2", target_bir_lowering=False, num_devices=1)
    arrays = {f"in_{k}": v for k, v in layout(inputs).items()}
    args = {k[3:]: nc.dram_tensor(k, v.shape, mybir.dt.from_np(v.dtype), kind="ExternalInput").ap()
            for k, v in arrays.items()}
    out = nc.dram_tensor("out_x", (NT, D), F32, kind="ExternalOutput").ap()
    program(nc, args, out)
    r = run_bass_kernel_spmd(nc, [arrays], core_ids=[0])
    return r.results[0]["out_x"].reshape(B, T, D)
```
